# Optimizing a Trainium2 kernel written in Bass

```python
import numpy as np
import jax
import jax.numpy as jnp

def _softmax(x, axis=-1):
    return jax.nn.softmax(x, axis=axis)

def _gelu(x):
    return jax.nn.gelu(x, approximate=True)

def _silu(x):
    return jax.nn.silu(x)

def _sigmoid(x):
    return jax.nn.sigmoid(x)

def _layernorm(x, axis=-1, eps=1e-05):
    m = jnp.mean(x, axis=axis, keepdims=True)
    v = jnp.var(x, axis=axis, keepdims=True)
    return (x - m) / jnp.sqrt(v + eps)

def _scatter_add(tgt, idx, src, axis=0):
    return tgt.at[idx].add(src)

def _segment_sum(src, seg, n):
    return jax.ops.segment_sum(src, seg, n)
kernel_name = 'mk_xattn_ffn_d2_seqx_r8_aa60d1'

def setup_inputs(seed: int=0):
    np.random.seed(seed)
    _w = jnp.asarray

    def _rec_inputs():
        import jax
        import jax.numpy as jnp
        _rk = jax.random.key(seed)
        x = -0.0002928 + 1 * jax.random.normal(jax.random.fold_in(_rk, 1), (64, 128, 128), jnp.float32)
        _lenS = 128 - jax.random.randint(jax.random.fold_in(_rk, 7), (64,), 0, max(1, 128 // 4) + 1, jnp.int32)
        _lenS2 = 77 - jax.random.randint(jax.random.fold_in(_rk, 8), (64,), 0, max(1, 77 // 4) + 1, jnp.int32)
        _ctx_1024P = jax.random.normal(jax.random.fold_in(_rk, 11), (64, 16, 128), jnp.float32)
        _ctx_1024c = jax.random.dirichlet(jax.random.fold_in(_rk, 511), 0.3 * jnp.ones((16,), jnp.float32), (64, 77))
        _ctx_1024t = jnp.einsum('bsk,bkd->bsd', _ctx_1024c, _ctx_1024P)
        _ctx_1024t = _ctx_1024t * jax.lax.rsqrt(jnp.mean(jnp.square(_ctx_1024t)) + 1e-12) * 0.953939
        ctx_1024 = -1.39393e-06 + 0.999914 * (_ctx_1024t + 0.3 * jax.random.normal(jax.random.fold_in(_rk, 611), (64, 77, 128), jnp.float32))
        _validS = jnp.arange(128)[None, :] < _lenS[:, None]
        _validS2 = jnp.arange(77)[None, :] < _lenS2[:, None]
        _causal = jnp.tril(jnp.ones((128, 128), dtype=bool))
        mask_BxSxS2_bk1 = jnp.broadcast_to(_validS2[:, None, :], (64, 128, 77))
        return (x, ctx_1024, mask_BxSxS2_bk1)
    x, ctx_1024, mask_BxSxS2_bk1 = _rec_inputs()

    def _L0_xattn_setup():
        import jax, jax.numpy as jnp
        import numpy as np
        DIM = 128
        NUM_HEADS = 16
        HEAD_DIM = DIM // NUM_HEADS
        SCALE = HEAD_DIM ** (-0.5)
        key = jax.random.key(seed)
        ks = jax.random.split(key, 8)
        B, QL, KL = (2, 256, 256)
        s = DIM ** (-0.5)
        return {'q': jax.random.normal(ks[0], (B, QL, DIM), jnp.float32), 'k': jax.random.normal(ks[1], (B, KL, DIM), jnp.float32), 'v': jax.random.normal(ks[2], (B, KL, DIM), jnp.float32), 'Wq': jax.random.normal(ks[3], (DIM, DIM), jnp.float32) * s, 'Wk': jax.random.normal(ks[4], (DIM, DIM), jnp.float32) * s, 'Wv': jax.random.normal(ks[5], (DIM, DIM), jnp.float32) * s, 'Wo': jax.random.normal(ks[6], (DIM, DIM), jnp.float32) * s, 'bo': jax.random.normal(ks[7], (DIM,), jnp.float32) * 0.02}
    _L0_xattn_all = _L0_xattn_setup()
    _L0_xattn_in = {k: v for k, v in _L0_xattn_all.items() if k in ('Wq', 'Wk', 'Wv', 'Wo', 'bo')}
    del _L0_xattn_all

    def _L0_ffn_setup():
        import jax, jax.numpy as jnp
        import numpy as np
        TEMPERATURE = 0.5
        CAPACITY_FACTOR = 1.25
        TOP_K = 1
        key = jax.random.key(seed)
        ks = jax.random.split(key, 5)
        B, S, D, H, E = (4, 256, 128, 256, 8)
        s = 0.02
        return {'x': jax.random.normal(ks[0], (B, S, D), jnp.float32), 'gate_w': jax.random.normal(ks[1], (E, D), jnp.float32) * s, 'gate_b': jnp.zeros((E,), jnp.float32), 'rms_w': jnp.ones((E,), jnp.float32), 'w1': jax.random.normal(ks[2], (E, D, H), jnp.float32) * s, 'b1': jnp.zeros((E, H), jnp.float32), 'w2': jax.random.normal(ks[3], (E, H, D), jnp.float32) * s, 'b2': jnp.zeros((E, D), jnp.float32)}
    _L0_ffn_all = _L0_ffn_setup()
    _L0_ffn_in = {k: v for k, v in _L0_ffn_all.items() if k in ('gate_w', 'gate_b', 'rms_w', 'w1', 'b1', 'w2', 'b2')}
    del _L0_ffn_all

    def _L1_xattn_setup():
        import jax, jax.numpy as jnp
        import numpy as np
        DIM = 128
        HEADS = 16
        DIM_HEAD = 64
        INNER = HEADS * DIM_HEAD
        B, N = (2, 256)
        key = jax.random.key(seed)
        ks = jax.random.split(key, 8)
        q = jax.random.normal(ks[0], (B, N, DIM), dtype=jnp.float32)
        k = jax.random.normal(ks[1], (B, N, DIM), dtype=jnp.float32)
        v = jax.random.normal(ks[2], (B, N, DIM), dtype=jnp.float32)
        causal = jnp.triu(jnp.ones((N, N), dtype=jnp.bool_), k=1)
        mask = jnp.broadcast_to(causal, (B, N, N))
        s = 0.02
        Wq = jax.random.normal(ks[3], (DIM, INNER), dtype=jnp.float32) * s
        Wk = jax.random.normal(ks[4], (DIM, INNER), dtype=jnp.float32) * s
        Wv = jax.random.normal(ks[5], (DIM, INNER), dtype=jnp.float32) * s
        Wo = jax.random.normal(ks[6], (INNER, DIM), dtype=jnp.float32) * s
        bo = jnp.zeros((DIM,), dtype=jnp.float32)
        return {'q': q, 'k': k, 'v': v, 'mask': mask, 'Wq': Wq, 'Wk': Wk, 'Wv': Wv, 'Wo': Wo, 'bo': bo}
    _L1_xattn_all = _L1_xattn_setup()
    _L1_xattn_in = {k: v for k, v in _L1_xattn_all.items() if k in ('Wq', 'Wk', 'Wv', 'Wo', 'bo')}
    del _L1_xattn_all

    def _L1_ffn_setup():
        import jax, jax.numpy as jnp
        import numpy as np
        DIM = 128
        HIDDEN = 512
        N_EXPERTS = 8
        K = 2
        TEMP = 1.0

        def _expert_ffn(xf, wa, ba, wb, bb):
            h = xf @ wa.T + ba
            h1, h2 = jnp.split(h, 2, axis=-1)
            h = jax.nn.silu(h1) * h2
            return h @ wb.T + bb
        key = jax.random.key(seed)
        ks = jax.random.split(key, 7)
        s = 0.02
        x = jax.random.normal(ks[0], (4, 256, DIM), dtype=jnp.float32)
        router_w = jax.random.normal(ks[1], (N_EXPERTS, DIM), dtype=jnp.float32) * s
        router_b = jnp.zeros((N_EXPERTS,), dtype=jnp.float32)
        w1 = jax.random.normal(ks[2], (N_EXPERTS, 2 * HIDDEN, DIM), dtype=jnp.float32) * s
        b1 = jnp.zeros((N_EXPERTS, 2 * HIDDEN), dtype=jnp.float32)
        w2 = jax.random.normal(ks[3], (N_EXPERTS, DIM, HIDDEN), dtype=jnp.float32) * s
        b2 = jnp.zeros((N_EXPERTS, DIM), dtype=jnp.float32)
        return {'x': x, 'router_w': router_w, 'router_b': router_b, 'w1': w1, 'b1': b1, 'w2': w2, 'b2': b2}
    _L1_ffn_all = _L1_ffn_setup()
    _L1_ffn_in = {k: v for k, v in _L1_ffn_all.items() if k in ('router_w', 'router_b', 'w1', 'b1', 'w2', 'b2')}
    del _L1_ffn_all
    return {'x': x, 'ctx_1024': ctx_1024, 'mask_BxSxS2_bk1': mask_BxSxS2_bk1, 'L0_xattn_Wq': _L0_xattn_in['Wq'], 'L0_xattn_Wk': _L0_xattn_in['Wk'], 'L0_xattn_Wv': _L0_xattn_in['Wv'], 'L0_xattn_Wo': _L0_xattn_in['Wo'], 'L0_xattn_bo': _L0_xattn_in['bo'], 'L0_ffn_gate_w': _L0_ffn_in['gate_w'], 'L0_ffn_gate_b': _L0_ffn_in['gate_b'], 'L0_ffn_rms_w': _L0_ffn_in['rms_w'], 'L0_ffn_w1': _L0_ffn_in['w1'], 'L0_ffn_b1': _L0_ffn_in['b1'], 'L0_ffn_w2': _L0_ffn_in['w2'], 'L0_ffn_b2': _L0_ffn_in['b2'], 'L1_xattn_Wq': _L1_xattn_in['Wq'], 'L1_xattn_Wk': _L1_xattn_in['Wk'], 'L1_xattn_Wv': _L1_xattn_in['Wv'], 'L1_xattn_Wo': _L1_xattn_in['Wo'], 'L1_xattn_bo': _L1_xattn_in['bo'], 'L1_ffn_router_w': _L1_ffn_in['router_w'], 'L1_ffn_router_b': _L1_ffn_in['router_b'], 'L1_ffn_w1': _L1_ffn_in['w1'], 'L1_ffn_b1': _L1_ffn_in['b1'], 'L1_ffn_w2': _L1_ffn_in['w2'], 'L1_ffn_b2': _L1_ffn_in['b2']}

def reference(x, ctx_1024, mask_BxSxS2_bk1, L0_xattn_Wq, L0_xattn_Wk, L0_xattn_Wv, L0_xattn_Wo, L0_xattn_bo, L0_ffn_gate_w, L0_ffn_gate_b, L0_ffn_rms_w, L0_ffn_w1, L0_ffn_b1, L0_ffn_w2, L0_ffn_b2, L1_xattn_Wq, L1_xattn_Wk, L1_xattn_Wv, L1_xattn_Wo, L1_xattn_bo, L1_ffn_router_w, L1_ffn_router_b, L1_ffn_w1, L1_ffn_b1, L1_ffn_w2, L1_ffn_b2):
    import jax
    import jax.numpy as jnp

    def _L0_xattn_ref(q, k, v, Wq, Wk, Wv, Wo, bo):
        import jax, jax.numpy as jnp
        import numpy as np
        DIM = 128
        NUM_HEADS = 16
        HEAD_DIM = DIM // NUM_HEADS
        SCALE = HEAD_DIM ** (-0.5)
        B, QL, _ = q.shape
        KL = k.shape[1]
        qh = (q @ Wq.T).reshape(B, QL, NUM_HEADS, HEAD_DIM)
        kh = (k @ Wk.T).reshape(B, KL, NUM_HEADS, HEAD_DIM)
        vh = (v @ Wv.T).reshape(B, KL, NUM_HEADS, HEAD_DIM)
        attn = jnp.einsum('bnhc,bmhc->bhnm', qh, kh) * SCALE
        attn = jax.nn.softmax(attn, axis=-1)
        out = jnp.einsum('bhnm,bmhc->bnhc', attn, vh).reshape(B, QL, DIM)
        return out @ Wo.T + bo

    def _L0_ffn_ref(x, gate_w, gate_b, rms_w, w1, b1, w2, b2):
        import jax, jax.numpy as jnp
        import numpy as np
        TEMPERATURE = 0.5
        CAPACITY_FACTOR = 1.25
        TOP_K = 1
        B, S, D = x.shape
        E = gate_w.shape[0]
        xf = x.reshape(-1, D)
        N = xf.shape[0]
        logits = xf @ gate_w.T + gate_b
        eps = jnp.finfo(logits.dtype).eps
        ms = jnp.mean(logits * logits, axis=-1, keepdims=True)
        logits = logits * jax.lax.rsqrt(ms + eps) * rms_w
        gates = jax.nn.softmax(logits / TEMPERATURE, axis=-1)
        g, idx = jax.lax.top_k(gates, TOP_K)
        g, idx = (g[:, 0], idx[:, 0])
        capacity = min(int(np.ceil(N * TOP_K / E * CAPACITY_FACTOR)), N)
        counts = jnp.zeros((E,), jnp.int32).at[idx].add(1)
        active = (counts > 0) & (capacity >= 1)
        mask = active[idx].astype(gates.dtype)
        masked = g * mask
        norm_g = masked / (masked + 1e-06)
        h = jax.nn.gelu(jnp.einsum('nd,edh->neh', xf, w1) + b1, approximate=False)
        y = jnp.einsum('neh,ehd->ned', h, w2) + b2
        out = (y * norm_g[:, None, None]).sum(axis=1)
        return out.reshape(B, S, D)

    def _L1_xattn_ref(q, k, v, mask, Wq, Wk, Wv, Wo, bo):
        import jax, jax.numpy as jnp
        import numpy as np
        DIM = 128
        HEADS = 16
        DIM_HEAD = 64
        INNER = HEADS * DIM_HEAD
        B, N = (2, 256)
        h, d = (HEADS, DIM_HEAD)
        scale = d ** (-0.5)
        b, n, _ = q.shape

        def heads_split(x):
            return x.reshape(b, -1, h, d).transpose(0, 2, 1, 3)
        qh = heads_split(q @ Wq)
        kh = heads_split(k @ Wk)
        vh = heads_split(v @ Wv)
        dots = jnp.einsum('bhid,bhjd->bhij', qh, kh) * scale
        mask_value = -jnp.finfo(dots.dtype).max
        dots = jnp.where(mask[:, None, :, :], mask_value, dots)
        attn = jax.nn.softmax(dots, axis=-1)
        out = jnp.einsum('bhij,bhjd->bhid', attn, vh)
        out = out.transpose(0, 2, 1, 3).reshape(b, n, h * d)
        out = out @ Wo + bo
        return out

    def _L1_ffn_ref(x, router_w, router_b, w1, b1, w2, b2):
        import jax, jax.numpy as jnp
        import numpy as np
        DIM = 128
        HIDDEN = 512
        N_EXPERTS = 8
        K = 2
        TEMP = 1.0

        def _expert_ffn(xf, wa, ba, wb, bb):
            h = xf @ wa.T + ba
            h1, h2 = jnp.split(h, 2, axis=-1)
            h = jax.nn.silu(h1) * h2
            return h @ wb.T + bb
        b, t, d = x.shape
        logits = (x @ router_w.T + router_b) / TEMP
        topk_val, topk_idx = jax.lax.top_k(logits, K)
        weights = jax.nn.softmax(topk_val, axis=-1)
        xf = x.reshape(-1, d)
        outs = jax.vmap(_expert_ffn, in_axes=(None, 0, 0, 0, 0))(xf, w1, b1, w2, b2)
        outs = jnp.transpose(outs, (1, 0, 2))
        idx = topk_idx.reshape(-1, K)
        gathered = jnp.take_along_axis(outs, idx[:, :, None], axis=1)
        combined = (gathered * weights.reshape(-1, K, 1)).sum(axis=1)
        return combined.reshape(b, t, d)
    x = x + _L0_xattn_ref(_layernorm(x, axis=-1), ctx_1024, ctx_1024, L0_xattn_Wq, L0_xattn_Wk, L0_xattn_Wv, L0_xattn_Wo, L0_xattn_bo)
    x = x + _L0_ffn_ref(_layernorm(x, axis=-1), L0_ffn_gate_w, L0_ffn_gate_b, L0_ffn_rms_w, L0_ffn_w1, L0_ffn_b1, L0_ffn_w2, L0_ffn_b2)
    x = x + _L1_xattn_ref(_layernorm(x, axis=-1), ctx_1024, ctx_1024, mask_BxSxS2_bk1, L1_xattn_Wq, L1_xattn_Wk, L1_xattn_Wv, L1_xattn_Wo, L1_xattn_bo)
    x = x + _L1_ffn_ref(_layernorm(x, axis=-1), L1_ffn_router_w, L1_ffn_router_b, L1_ffn_w1, L1_ffn_b1, L1_ffn_w2, L1_ffn_b2)
    return x

_drawn_inputs = setup_inputs


def setup_inputs(seed=0):
    import zlib

    import numpy as np

    out = dict(_drawn_inputs(seed))
    spreads = {'L0_ffn_gate_b': (0.0, 2.0),
     'L0_ffn_rms_w': (1.0, 0.6),
     'L0_ffn_b1': (0.0, 0.1),
     'L0_ffn_b2': (0.0, 0.1),
     'L1_xattn_bo': (0.0, 0.1),
     'L1_ffn_router_b': (0.0, 0.1),
     'L1_ffn_b1': (0.0, 0.8),
     'L1_ffn_b2': (0.0, 0.484)}
    factors = {'L0_xattn_bo': 2.952,
     'L0_ffn_gate_w': 64.0,
     'L1_xattn_Wq': 8.0,
     'L1_xattn_Wk': 8.0,
     'L1_ffn_w1': 6.839,
     'L1_ffn_w2': 6.717}
    for name, (base, spread) in spreads.items():
        noise = np.random.default_rng([zlib.crc32(name.encode()), seed]).standard_normal(out[name].shape)
        drawn = base * np.exp(spread * noise) if base else spread * noise
        out[name] = jnp.asarray(drawn.astype(out[name].dtype))
    for name, factor in factors.items():
        out[name] = (out[name] * factor).astype(out[name].dtype)
    return out
```

```python
from contextlib import ExitStack

import concourse.bass as bass
from concourse import mybir

F32 = mybir.dt.float32
F32R = mybir.dt.float32r
BF16 = mybir.dt.bfloat16
U8 = mybir.dt.uint8
ALU = mybir.AluOpType
ACT = mybir.ActivationFunctionType
AX = mybir.AxisListType

P = 128
NB = 64
KL = 77
NH = 16
GB = 4
NG = NB // GB
UH = 8
UPG = 2 * GB
EPS = 1e-5
NE = 8
MASKED = -3.3895313892515355e38


def need(eng, sem, value):
    if not (isinstance(value, int) and value <= 0):
        eng.wait_ge(sem, value)


def split(nc, hi, lo, full, sem, at):
    nc.vector.tensor_copy(hi, full).then_inc(sem, 1)
    nc.vector.wait_ge(sem, at + 1)
    nc.vector.tensor_tensor(lo, full, hi.bitcast(F32), ALU.subtract).then_inc(sem, 1)
    return at + 2


def passes(nc, out, left, right, start=True, stop=True):
    nc.tensor.matmul(out, left[0], right[0], start=start, stop=False)
    nc.tensor.matmul(out, left[0], right[1], start=False, stop=False)
    return nc.tensor.matmul(out, left[1], right[0], start=False, stop=stop)


class Constants:

    def __init__(self, nc, ctx, ident_in):
        def sb(name, shape, dt):
            return ctx.enter_context(nc.sbuf_tensor(name, shape, dt))

        self.ident = sb("ident", [P, P], F32)
        self.ident_bf = sb("ident_bf", [P, P], BF16)
        self.ones_row = sb("ones_row", [1, P], F32R)
        self.minus_half = sb("minus_half", [P, GB], F32)
        ident_loaded = ctx.enter_context(nc.semaphore("ident_loaded"))
        const_made = ctx.enter_context(nc.semaphore("const_made"))
        self.passed = ctx.enter_context(nc.semaphore("passed"))
        with nc.Block() as block:
            @block.sync
            def _(sp):
                sp.dma_start(self.ident[:], ident_in).then_inc(ident_loaded, 16)
                sp.wait_ge(ident_loaded, 16)

            @block.vector
            def _(dve):
                nc.vector.memset(self.ones_row[:].bitcast(F32), 1.0).then_inc(const_made, 1)
                nc.vector.memset(self.minus_half[:], -0.5).then_inc(const_made, 1)
                dve.wait_ge(ident_loaded, 16)
                nc.vector.tensor_copy(self.ident_bf[:], self.ident[:]).then_inc(const_made, 1)
                dve.wait_ge(const_made, 3)


def wait_apart(eng, const, sem, value):
    need(eng, sem, value)
    if not isinstance(value, int):
        eng.sem_inc(const.passed, 1)


class Norm:

    def __init__(self, nc, tag, sb, sem, const, X, bufs):
        self.nc, self.X, self.const = nc, X, const
        self.stats = sb("stats", [P, GB, 6], F32)
        self.mv = sb("mv", [P, GB, 2], F32)
        self.ve = sb("ve", [P, GB], F32)
        self.rstd = sb("rstd", [P, GB], F32)
        self.xn = sb("xn", [P, bufs, GB, P], F32)
        self.step = sem("ln_step")
        self.rstd_done = sem("rstd_done")
        self.xn_done = sem("xn_done")

    def on_dve(self, dve, g, par):
        nc, n = self.nc, g * (2 * GB + 1)
        for j in range(GB):
            nc.vector.bn_stats(self.stats[:, j, :], self.X[:, g * GB + j, :]).then_inc(self.step, 1)
        for j in range(GB):
            wait_apart(dve, self.const, self.step, n + j + 1)
            nc.vector.bn_aggr(self.mv[:, j, :], self.stats[:, j, :]).then_inc(self.step, 1)
        dve.wait_ge(self.step, n + 2 * GB)
        nc.vector.tensor_scalar(self.ve[:], self.mv[:, :, 1], EPS, None, ALU.add).then_inc(self.step, 1)
        dve.wait_ge(self.rstd_done, g + 1)
        for j in range(GB):
            nc.vector.tensor_scalar(self.xn[:, par, j, :], self.X[:, g * GB + j, :], self.mv[:, j, 0:1],
                                    self.rstd[:, j:j + 1], ALU.subtract, ALU.mult).then_inc(self.xn_done, 1)

    def on_pool(self, pool, g):
        pool.wait_ge(self.step, (g + 1) * (2 * GB + 1))
        self.nc.gpsimd.tensor_tensor(self.rstd[:], self.ve[:], self.const.minus_half[:],
                                     ALU.pow).then_inc(self.rstd_done, 1)


def attention(nc, const, X, layer, x_in, ctx_in, mask_in, wq, wk, wv, wo, bo, signs):
    small = layer == 0
    DH = 8 if small else 64
    INNER = NH * DH
    SCALE = float(DH) ** -0.5
    VW = DH + 1
    QC = 4 if small else 8
    KW = GB * KL
    KBW = 4 * KL if small else 2 * KL
    CPB = 1 if small else 2
    NV = 1 if small else 2 * GB
    NOT = 1 if small else 2
    OC = INNER // P
    tag = f"L{layer}_"

    FRONT = [("xt", 0), ("ct", 0)] + [("q", c) for c in range(QC)] + [("k", c) for c in range(QC)] \
        + [("v", c) for c in range(NV)]
    LATER = -(-(len(FRONT) - 2) // (UPG - 2))

    def front_of(step):
        if step == UPG - 1:
            return []
        return FRONT[:2] if step == 0 else FRONT[2 + (step - 1) * LATER:2 + step * LATER]

    BODY = 2 * (len(FRONT) + 2 * UPG + GB * (NOT + 1))
    FIRST = len(FRONT) + BODY - (NOT + 1)
    assert BODY % 2 == 0

    with ExitStack() as ctx:
        def sb(name, shape, dt):
            return ctx.enter_context(nc.sbuf_tensor(tag + name, shape, dt))

        def sem(name):
            return ctx.enter_context(nc.semaphore(tag + name))

        S = ctx.enter_context(nc.psum_tensor(tag + "S", [P, 2, 2, 512], F32))
        PT = ctx.enter_context(nc.psum_tensor(tag + "PT", [P, 2, 512], F32))
        R = ctx.enter_context(nc.psum_tensor(tag + "R", [P, 2, 512], F32))

        WQ = [sb(f"WQ{i}", [P, QC * P], F32R) for i in range(2)]
        WK = [sb(f"WK{i}", [P, QC * P], F32R) for i in range(2)]
        WV = [sb(f"WV{i}", [P, INNER], F32R) for i in range(2)]
        WO = [sb(f"WO{i}", [P, OC * P], F32R) for i in range(2)]
        BO = [sb(f"BO{i}", [1, P], F32R) for i in range(2)]
        bo_raw = sb("bo_raw", [1, P], F32)
        norm = Norm(nc, tag, sb, sem, const, X, 1)
        cx = sb("cx", [KL, GB, P], F32)
        xT = [sb(f"xT{i}", [P, GB * P], F32R) for i in range(2)]
        cT = [sb(f"cT{i}", [P, KW], F32R) for i in range(2)]
        QD = F32R if small else F32
        qT = sb("qT", [P, 2, QC, GB * P], QD)
        kbd = sb("kbd", [P, 2, QC, GB, KBW], QD)
        Sm = sb("Sm", [P, 2, UH, KL], F32)
        if small:
            sgn = sb("sgn", [P, 2], F32)
            rounded = sb("rounded", [P, 2, GB * P], F32R)
            kst = sb("kst", [P, 2, KW], F32R)
            raw = Sm[:].rearrange("p a h k -> p (a h k)")
        else:
            mk = sb("mk", [P, 2, GB, KL], U8)
            mb = sb("mb", [P, 2, GB, KL], BF16)
            raw = kbd[:].rearrange("p a c b k -> p (a c b k)")
        V = sb("V", [KL, 2, GB, NH, VW], F32)
        nmax = sb("nmax", [P, 2, UH], F32)
        PTs = sb("PTs", [KL, 2, 512], F32)
        rden = sb("rden", [P, 2, 4], F32)
        O = sb("O", [P, 2, NH, DH], F32)
        OT = [sb(f"OT{i}", [P, OC * P], F32R) for i in range(2)]

        w_loaded = sem("w_loaded")
        prepared = sem("prepared")
        ready = sem("ready")
        x_loaded = [sem(f"x_loaded{i}") for i in range(2)]
        ctx_loaded = sem("ctx_loaded")
        mask_loaded = [sem(f"mask_loaded{i}") for i in range(2)]
        ring_full = [sem(f"ring_full{i}") for i in range(2)]
        ring_done = [sem(f"ring_done{i}") for i in range(2)]
        xt_hi = sem("xt_hi")
        ct_hi = sem("ct_hi")
        qk_hi = sem("qk_hi")
        kbd_done = sem("kbd_done")
        mask_done = sem("mask_done")
        s_full = sem("s_full")
        max_done = sem("max_done")
        sub_done = sem("sub_done")
        exp_done = sem("exp_done")
        pt_full = sem("pt_full")
        pt_done = sem("pt_done")
        rec_done = sem("rec_done")
        ot_hi = sem("ot_hi")
        x_done = sem("x_done")

        Vrows = V[:].rearrange("p a b h w -> p a (b h) w")

        def walk(eng, do, exp_after_transposes=False):
            job = [0, 0]

            def take():
                job[0] += 1
                return (job[0] - 1) % 2, job[1] + (job[0] - 1) // 2

            def pair(h, first, last):
                done = {}
                for par in range(2):
                    for st in range(UPG):
                        g, u = 2 * h + par, (2 * h + par) * UPG + st
                        final = last and par == 1
                        nst, npar = (st + 1) % UPG, (par + (st + 1) // UPG) % 2
                        more = not (final and st == UPG - 1)
                        if more and not exp_after_transposes:
                            do.scores(u + 1, nst, npar, g + 1 if nst == 0 else g)
                        do.transposes(u, st)
                        if more and exp_after_transposes:
                            do.scores(u + 1, nst, npar, g + 1 if nst == 0 else g)
                        if not final:
                            for kind, c in front_of(st):
                                do.front(kind, c, g + 1, 1 - par, h + par, take())
                        for cc in range(2):
                            do.values(u, st, par, cc, take())
                        if st % 2 == 0 and not (first and par == 0 and st == 0):
                            for c in range(NOT):
                                do.outT(g * GB + st // 2 - 1, (st // 2 - 1) % 2, c, take())
                            do.out(g * GB + st // 2 - 1, take())
                        if st == UPG - 1 and not last:
                            do.norm(g + 2, par, h + 1)

            do.norm(0, 0, 0)
            for kind, c in FRONT:
                do.front(kind, c, 0, 0, 0, take())
            do.scores(0, 0, 0, 0)
            do.norm(1, 1, 0)
            pair(0, True, False)
            assert job[0] == FIRST
            with eng.Fori(1, NG // 2 - 1) as h:
                job[:] = [FIRST, (h - 1) * (BODY // 2)]
                pair(h, False, False)
            job[:] = [FIRST + (NG // 2 - 2) * BODY, 0]
            pair(NG // 2 - 1, False, True)
            for c in range(NOT):
                do.outT(NB - 1, 1, c, take())
            do.out(NB - 1, take())

        def before(job, k):
            bank, n = job
            return (bank, n - k // 2) if k % 2 == 0 else ((1, n - k // 2 - 1) if bank == 0 else (0, n - k // 2))

        with nc.Block() as block:
            @block.sync
            def _(sp):
                for t, w in enumerate((wq, wk, wv, wo)):
                    dst = raw[:, t * INNER:(t + 1) * INNER]
                    if t == 3 and not small:
                        dst = dst.rearrange("p (c d) -> p c d", c=OC)
                        w = w.rearrange("(c p) d -> p c d", p=P)
                    sp.dma_start(dst, w).then_inc(w_loaded, 16)
                sp.dma_start(bo_raw[:], bo.unsqueeze(0)).then_inc(w_loaded, 16)
                if small:
                    sp.dma_start(sgn[:], signs).then_inc(w_loaded, 16)

                def load(g, par):
                    if x_in is not None:
                        sp.dma_start(X[:, bass.ds(g * GB, GB), :],
                                     x_in[bass.ds(g * GB, GB)].rearrange("b s d -> s b d")
                                     ).then_inc(x_loaded[par], 16)
                    if not small:
                        wait_apart(sp, const, mask_done, g - 1)
                        sp.dma_start(mk[:, par], mask_in[bass.ds(g * GB, GB)].rearrange("b s k -> s b k")
                                     ).then_inc(mask_loaded[par], 16)
                    wait_apart(sp, const, ct_hi, g)
                    sp.dma_start(cx[:], ctx_in[bass.ds(g * GB, GB)].rearrange("b k d -> k b d")
                                 ).then_inc(ctx_loaded, 16)

                load(0, 0)
                load(1, 1)
                with sp.Fori(1, NG // 2) as h:
                    for par in range(2):
                        load(2 * h + par, par)

            @block.gpsimd
            def _(pool):
                class do:
                    @staticmethod
                    def front(kind, c, g, par, h, job):
                        bank, n = job
                        if kind == "ct" and not small:
                            pool.wait_ge(mask_loaded[par], 16 * h + 16)
                            wait_apart(pool, const, s_full, UPG * (g - 1))
                            nc.gpsimd.tensor_scalar(mb[:, par], mk[:, par], MASKED, None,
                                                    ALU.mult).then_inc(mask_done, 1)
                        if kind == "k" and small:
                            wait_apart(pool, const, ring_done[bank], n + 1)
                            for r in range(4):
                                rows = slice(32 * r, 32 * r + 32)
                                nc.gpsimd.tensor_copy(
                                    kbd[rows, par, c, :, r * KL:(r + 1) * KL],
                                    kst[rows, bank, :].rearrange("p (b k) -> p b k", b=GB)).then_inc(kbd_done, 1)

                    @staticmethod
                    def norm(g, par, h):
                        norm.on_pool(pool, g)

                    scores = transposes = values = outT = out = staticmethod(lambda *a: None)

                pool.wait_ge(ready, 2)
                walk(pool, do)

            @block.scalar
            def _(act):
                class do:
                    @staticmethod
                    def front(kind, c, g, par, h, job):
                        bank, n = job
                        if kind == "q" and not small:
                            return
                        act.wait_ge(ring_full[bank], n + 1)
                        if kind == "xt":
                            nc.scalar.copy(xT[0][:], R[:, bank, :]).then_inc(xt_hi, 1)
                        elif kind == "ct":
                            nc.scalar.copy(cT[0][:], R[:, bank, 0:KW]).then_inc(ct_hi, 1)
                        elif kind == "q":
                            nc.scalar.copy(rounded[:, bank, :], R[:, bank, :]).then_inc(qk_hi, 1)
                        elif kind == "k" and small:
                            nc.scalar.copy(rounded[:, bank, 0:KW], R[:, bank, 0:KW]).then_inc(qk_hi, 1)
                        elif kind == "k":
                            for r in range(2):
                                rows = slice(64 * r, 64 * r + 64)
                                last = nc.scalar.copy(kbd[rows, par, c, :, r * KL:(r + 1) * KL],
                                                      R[rows, bank, 0:KW].rearrange("p (b k) -> p b k", b=GB))
                            last.then_inc(ring_done[bank], 1)
                        elif small:
                            nc.scalar.copy(Vrows[:, par, :, 0:DH],
                                           R[0:KL, bank, :].rearrange("p (h w) -> p h w", w=DH)
                                           ).then_inc(ring_done[bank], 1)
                        else:
                            nc.scalar.copy(Vrows[:, par, UH * c:UH * (c + 1), 0:DH],
                                           R[0:KL, bank, :].rearrange("p (h w) -> p h w", w=DH)
                                           ).then_inc(ring_done[bank], 1)

                    @staticmethod
                    def scores(u, st, par, g):
                        act.wait_ge(sub_done, u + 1)
                        s = Sm[:, st % 2].rearrange("p h k -> p (h k)")
                        nc.scalar.activation(s, s, ACT.Exp, scale=SCALE).then_inc(exp_done, 1)

                    @staticmethod
                    def transposes(u, st):
                        for cc in range(2):
                            act.wait_ge(pt_full, 2 * u + cc + 1)
                            nc.scalar.copy(PTs[:, cc, :], PT[0:KL, cc, :]).then_inc(pt_done, 1)

                    values = staticmethod(lambda *a: None)

                    @staticmethod
                    def outT(sq, bp, c, job):
                        bank, n = job
                        w = INNER // NOT
                        act.wait_ge(ring_full[bank], n + 1)
                        nc.scalar.copy(OT[0][:, c * w:(c + 1) * w], R[:, bank, 0:w]).then_inc(ot_hi, 1)

                    out = norm = staticmethod(lambda *a: None)

                act.wait_ge(ready, 2)
                walk(act, do, exp_after_transposes=True)

            @block.vector
            def _(dve):
                dve.wait_ge(w_loaded, (6 if small else 5) * 16)
                at = 0
                if small:
                    tmp = qT[:].rearrange("p a c t -> p (a c t)")
                    for W, t, lows in ((WQ, 0, (0, 0, 1, 1)), (WK, 1, (0, 1, 0, 1))):
                        parts = [tmp[:, (2 * t + i) * P:(2 * t + i + 1) * P] for i in range(2)]
                        at = split(nc, parts[0], parts[1], raw[:, t * INNER:(t + 1) * INNER], prepared, at)
                        dve.wait_ge(prepared, at)
                        for i in range(2):
                            for dup in range(4):
                                nc.vector.tensor_scalar(
                                    W[i][:].rearrange("p (h k c) -> p h k c", k=4, c=DH)[:, :, dup, :],
                                    parts[i].bitcast(F32).rearrange("p (h c) -> p h c", c=DH),
                                    -1.0 if lows[dup] else 1.0, None, ALU.mult).then_inc(prepared, 1)
                                at += 1
                    todo = ((WV, 2), (WO, 3))
                else:
                    todo = ((WQ, 0), (WK, 1), (WV, 2), (WO, 3))
                for W, t in todo:
                    at = split(nc, W[0][:], W[1][:], raw[:, t * INNER:(t + 1) * INNER], prepared, at)
                at = split(nc, BO[0][:], BO[1][:], bo_raw[:], prepared, at)
                dve.wait_ge(prepared, at)
                nc.vector.memset(kbd[:].rearrange("p a c b k -> p (a c b k)").bitcast(F32), 0.0).then_inc(ready, 1)
                nc.vector.memset(V[:].rearrange("p a b h w -> p (a b h) w")[:, :, DH:VW], 1.0).then_inc(ready, 1)
                dve.wait_ge(ready, 2)

                class do:
                    @staticmethod
                    def front(kind, c, g, par, h, job):
                        bank, n = job
                        if kind == "xt":
                            dve.wait_ge(xt_hi, g + 1)
                            nc.vector.tensor_tensor(xT[1][:], R[:, bank, :], xT[0][:].bitcast(F32),
                                                    ALU.subtract).then_inc(ring_done[bank], 1)
                        elif kind == "ct":
                            dve.wait_ge(ct_hi, g + 1)
                            nc.vector.tensor_tensor(cT[1][:], R[:, bank, 0:KW], cT[0][:].bitcast(F32),
                                                    ALU.subtract).then_inc(ring_done[bank], 1)
                        elif kind == "q" and small:
                            dve.wait_ge(qk_hi, 2 * QC * g + c + 1)
                            nc.vector.scalar_tensor_tensor(qT[:, par, c, :], R[:, bank, :], sgn[:, 0:1],
                                                           rounded[:, bank, :].bitcast(F32), ALU.mult,
                                                           ALU.subtract).then_inc(ring_done[bank], 1)
                        elif kind == "q":
                            dve.wait_ge(ring_full[bank], n + 1)
                            nc.vector.tensor_copy(qT[:, par, c, :], R[:, bank, :]).then_inc(ring_done[bank], 1)
                        elif kind == "k" and small:
                            dve.wait_ge(qk_hi, 2 * QC * g + QC + c + 1)
                            need(dve, kbd_done, 4 * (QC * g + c - 1))
                            nc.vector.scalar_tensor_tensor(kst[:, bank, :], R[:, bank, 0:KW], sgn[:, 1:2],
                                                           rounded[:, bank, 0:KW].bitcast(F32), ALU.mult,
                                                           ALU.subtract).then_inc(ring_done[bank], 1)

                    @staticmethod
                    def norm(g, par, h):
                        if x_in is not None:
                            dve.wait_ge(x_loaded[par], 16 * h + 16)
                        norm.on_dve(dve, g, 0)

                    @staticmethod
                    def scores(u, st, par, g):
                        dve.wait_ge(s_full, u + 1)
                        s = S[:, st % 2, :, 0:4 * KL].rearrange("p b (h k) -> p b h k", h=4)
                        nc.vector.tensor_reduce(nmax[:, st % 2, :].rearrange("p (b h) -> p b h", b=2), s,
                                                AX.X, ALU.max).then_inc(max_done, 1)
                        dve.wait_ge(max_done, u + 1)
                        nc.vector.tensor_tensor(
                            Sm[:, st % 2].rearrange("p (b h) k -> p b h k", b=2), s,
                            nmax[:, st % 2, :].rearrange("p (b h) -> p b h", b=2).unsqueeze(3).to_broadcast([P, 2, 4, KL]),
                            ALU.subtract).then_inc(sub_done, 1)

                    transposes = staticmethod(lambda *a: None)

                    @staticmethod
                    def values(u, st, par, cc, job):
                        bank, n = job
                        dve.wait_ge(ring_full[bank], n + 1)
                        o = R[:, bank, 0:4 * VW].rearrange("p (h w) -> p h w", w=VW)
                        nc.vector.reciprocal(rden[:, cc, :], o[:, :, DH]).then_inc(rec_done, 1)
                        dve.wait_ge(rec_done, 2 * u + cc + 1)
                        h0 = UH * (st % 2) + 4 * cc
                        nc.vector.tensor_tensor(O[:, (st // 2) % 2, h0:h0 + 4, :], o[:, :, 0:DH],
                                                rden[:, cc, :].unsqueeze(2).to_broadcast([P, 4, DH]),
                                                ALU.mult).then_inc(ring_done[bank], 1)

                    @staticmethod
                    def outT(sq, bp, c, job):
                        bank, n = job
                        w = INNER // NOT
                        dve.wait_ge(ot_hi, sq * NOT + c + 1)
                        nc.vector.tensor_tensor(OT[1][:, c * w:(c + 1) * w], R[:, bank, 0:w],
                                                OT[0][:, c * w:(c + 1) * w].bitcast(F32),
                                                ALU.subtract).then_inc(ring_done[bank], 1)

                    @staticmethod
                    def out(sq, job):
                        bank, n = job
                        dve.wait_ge(ring_full[bank], n + 1)
                        nc.vector.tensor_tensor(X[:, sq, :], R[:, bank, 0:P], X[:, sq, :],
                                                ALU.add).then_inc(ring_done[bank], 1)

                walk(dve, do)

            @block.tensor
            def _(pe):
                seen = {}

                def wait_job(job):
                    pe.wait_ge(ring_done[job[0]], job[1] + 1)

                class do:
                    @staticmethod
                    def front(kind, c, g, par, h, job):
                        bank, n = job
                        seen[kind] = job
                        need(pe, ring_done[bank], n)
                        if kind == "xt":
                            pe.wait_ge(norm.xn_done, GB * (g + 1))
                            for j in range(GB):
                                last = pe.transpose(R[:, bank, j * P:(j + 1) * P], norm.xn[:, 0, j, :],
                                                    const.ident[:])
                        elif kind == "ct":
                            pe.wait_ge(ctx_loaded, 16 * g + 16)
                            for j in range(GB):
                                last = pe.transpose(R[:, bank, j * KL:(j + 1) * KL], cx[:, j, :],
                                                    const.ident[0:KL, 0:KL])
                        elif kind == "q":
                            if c == 0:
                                wait_job(seen["xt"])
                            w = [W[:, c * P:(c + 1) * P] for W in WQ]
                            last = passes(nc, R[:, bank, :], w, [x[:] for x in xT])
                        elif kind == "k":
                            if c == 0:
                                wait_job(seen["ct"])
                            w = [W[:, c * P:(c + 1) * P] for W in WK]
                            last = passes(nc, R[:, bank, 0:KW], w, [x[:] for x in cT])
                        elif small:
                            for j in range(GB):
                                ct = [x[:, j * KL:(j + 1) * KL] for x in cT]
                                last = passes(nc, R[0:KL, bank, j * P:(j + 1) * P], ct, [W[:] for W in WV])
                        else:
                            ct = [x[:, (c // 2) * KL:(c // 2 + 1) * KL] for x in cT]
                            last = passes(nc, R[0:KL, bank, :], ct,
                                          [W[:, (c % 2) * 512:(c % 2 + 1) * 512] for W in WV])
                        last.then_inc(ring_full[bank], 1)

                    @staticmethod
                    def scores(u, st, par, g):
                        if st == 0:
                            wait_job(seen["v"])
                            wait_job(before(seen["v"], 1))
                            if small:
                                pe.wait_ge(kbd_done, 4 * QC * (g + 1))
                            else:
                                pe.wait_ge(mask_done, g + 1)
                        j, half = st // 2, st % 2
                        for b in range(2):
                            if not small:
                                pe.matmul(S[:, half, b, 0:4 * KL], const.ident_bf[:],
                                          mb[:, par, j, :].unsqueeze(1).to_broadcast([P, 4, KL]),
                                          start=True, stop=False, skip_group_check=True)
                            for i in range(CPB):
                                c = (2 * half + b) * CPB + i
                                last = pe.matmul(S[:, half, b, i * KBW:(i + 1) * KBW],
                                                 qT[:, par, c, j * P:(j + 1) * P], kbd[:, par, c, j, :],
                                                 start=small, stop=True, skip_group_check=not small)
                        last.then_inc(s_full, 1)

                    @staticmethod
                    def transposes(u, st):
                        pe.wait_ge(exp_done, u + 1)
                        for cc in range(2):
                            for k in range(4):
                                last = pe.transpose(PT[0:KL, cc, k * P:(k + 1) * P], Sm[:, st % 2, 4 * cc + k, :],
                                                    const.ident[:])
                            last.then_inc(pt_full, 1)

                    @staticmethod
                    def values(u, st, par, cc, job):
                        bank, n = job
                        seen["o", cc] = job
                        need(pe, ring_done[bank], n)
                        pe.wait_ge(pt_done, 2 * u + cc + 1)
                        for k in range(4):
                            last = pe.matmul(R[:, bank, k * VW:(k + 1) * VW], PTs[:, cc, k * P:(k + 1) * P],
                                             V[:, par, st // 2, UH * (st % 2) + 4 * cc + k, :],
                                             start=True, stop=True)
                        last.then_inc(ring_full[bank], 1)

                    @staticmethod
                    def outT(sq, bp, c, job):
                        bank, n = job
                        seen["ot", c] = job
                        need(pe, ring_done[bank], n)
                        if isinstance(sq, int) and sq == NB - 1:
                            wait_job(seen["o", 1])
                        for k in range(OC // NOT):
                            ch = c * (OC // NOT) + k
                            o = O[:, bp].rearrange("p h w -> p (h w)")[:, ch * P:(ch + 1) * P]
                            last = pe.transpose(R[:, bank, k * P:(k + 1) * P], o, const.ident[:])
                        last.then_inc(ring_full[bank], 1)

                    @staticmethod
                    def out(sq, job):
                        bank, n = job
                        need(pe, ring_done[bank], n)
                        for c in range(NOT):
                            wait_job(seen["ot", c])
                        y = R[:, bank, 0:P]
                        for ch in range(OC):
                            passes(nc, y, [x[:, ch * P:(ch + 1) * P] for x in OT],
                                   [W[:, ch * P:(ch + 1) * P] for W in WO], start=ch == 0, stop=False)
                        pe.matmul(y, const.ones_row[:], BO[0][:], start=False, stop=False)
                        pe.matmul(y, const.ones_row[:], BO[1][:], start=False, stop=True
                                  ).then_inc(ring_full[bank], 1)

                    norm = staticmethod(lambda *a: None)

                pe.wait_ge(ready, 2)
                walk(pe, do)


def normalise_all(nc, const, X, layer, XT, LG, gate_w, gate_b):
    tag = f"N{layer}_"
    with ExitStack() as ctx:
        def sb(name, shape, dt):
            return ctx.enter_context(nc.sbuf_tensor(tag + name, shape, dt))

        def sem(name):
            return ctx.enter_context(nc.semaphore(tag + name))

        T = ctx.enter_context(nc.psum_tensor(tag + "T", [P, 2, 512], F32))
        L = ctx.enter_context(nc.psum_tensor(tag + "L", [P, 2, 512], F32))
        U = ctx.enter_context(nc.psum_tensor(tag + "U", [P, 2, 512], F32))
        norm = Norm(nc, tag, sb, sem, const, X, 2)
        gw_raw = sb("gw_raw", [P, P], F32)
        GW = [sb(f"GW{i}", [P, P], F32R) for i in range(2)]
        gb = sb("gb", [NE, 1], F32)
        lgT = sb("lgT", [NE, 2, 512], F32)
        cleared = sem("cleared")
        gate_loaded = sem("gate_loaded")
        prepared = sem("prepared")
        t_full = sem("t_full")
        hi_done = sem("hi_done")
        lo_done = sem("lo_done")
        l_full = sem("l_full")
        l_done = sem("l_done")
        u_full = sem("u_full")
        u_done = sem("u_done")

        with nc.Block() as block:
            @block.sync
            def _(sp):
                sp.wait_ge(cleared, 1)
                sp.dma_start(gw_raw[:, 0:NE], gate_w).then_inc(gate_loaded, 16)
                sp.dma_start(gb[:], gate_b.unsqueeze(1)).then_inc(gate_loaded, 16)

            @block.gpsimd
            def _(pool):
                with pool.Fori(0, NG) as g:
                    norm.on_pool(pool, g)

            def pairs(eng, first, body, last):
                first()
                with eng.Fori(0, NG // 2 - 1) as h:
                    for par in range(2):
                        body(2 * h + par, par, True)
                body(NG - 2, 0, True)
                body(NG - 1, 1, False)
                last()

            @block.vector
            def _(dve):
                nc.vector.memset(gw_raw[:], 0.0).then_inc(cleared, 1)
                dve.wait_ge(gate_loaded, 32)
                split(nc, GW[0][:], GW[1][:], gw_raw[:], prepared, 0)

                def to_lg(g, par):
                    dve.wait_ge(u_full, g + 1)
                    nc.vector.tensor_copy(LG[:, bass.ds(g * GB, GB), :],
                                          U[:, par, 0:GB * NE].rearrange("p (b e) -> p b e", e=NE)
                                          ).then_inc(u_done, 1)

                def body(g, par, more):
                    if more:
                        norm.on_dve(dve, g + 1, 1 - par)
                    dve.wait_ge(hi_done, g + 1)
                    nc.vector.tensor_tensor(XT[1][:, bass.ds(g * 512, 512)], T[:, par, :],
                                            XT[0][:, bass.ds(g * 512, 512)].bitcast(F32),
                                            ALU.subtract).then_inc(lo_done, 1)
                    to_lg(g, par)

                pairs(dve, lambda: norm.on_dve(dve, 0, 0), body, lambda: None)
                dve.wait_ge(u_done, NG)

            @block.scalar
            def _(act):
                def body(g, par, more):
                    wait_apart(act, const, t_full, g + 1)
                    nc.scalar.copy(XT[0][:, bass.ds(g * 512, 512)], T[:, par, :]).then_inc(hi_done, 1)
                    act.wait_ge(l_full, g + 1)
                    nc.scalar.activation(lgT[:, par, :], L[0:NE, par, :], ACT.Identity, bias=gb[:]
                                         ).then_inc(l_done, 1)

                act.wait_ge(gate_loaded, 32)
                pairs(act, lambda: None, body, lambda: None)

            @block.tensor
            def _(pe):
                def tiles(g, par):
                    pe.wait_ge(norm.xn_done, GB * (g + 1))
                    for j in range(GB):
                        last = pe.transpose(T[:, par, j * P:(j + 1) * P], norm.xn[:, par, j, :], const.ident[:])
                    last.then_inc(t_full, 1)

                def body(g, par, more):
                    pe.wait_ge(lo_done, g + 1)
                    passes(nc, L[:, par, :], [W[:] for W in GW],
                           [x[:, bass.ds(g * 512, 512)] for x in XT]).then_inc(l_full, 1)
                    if more:
                        tiles(g + 1, 1 - par)
                    wait_apart(pe, const, l_done, g + 1)
                    for j in range(GB):
                        last = pe.transpose(U[:, par, j * NE:(j + 1) * NE], lgT[:, par, j * P:(j + 1) * P],
                                            const.ident[0:NE, 0:NE])
                    last.then_inc(u_full, 1)

                pe.wait_ge(prepared, 2)
                pairs(pe, lambda: tiles(0, 0), body, lambda: None)


def gate_scale(nc, LG, scale, gate_scale_in):
    N = NB * NE
    tag = "G_"
    with ExitStack() as ctx:
        def sb(name, shape):
            return ctx.enter_context(nc.sbuf_tensor(tag + name, shape, F32))

        rw = sb("rw", [P, NE])
        t = sb("t", [P, NB, NE])
        m = sb("m", [P, NB])
        r = sb("r", [P, NB])
        half = sb("half", [P, NB])
        loaded = ctx.enter_context(nc.semaphore(tag + "loaded"))
        v = ctx.enter_context(nc.semaphore(tag + "v"))
        a = ctx.enter_context(nc.semaphore(tag + "a"))
        q = ctx.enter_context(nc.semaphore(tag + "q"))
        wide = [P, NB, NE]

        with nc.Block() as block:
            @block.sync
            def _(sp):
                sp.dma_start(rw[:], gate_scale_in.partition_broadcast(P)).then_inc(loaded, 16)

            @block.gpsimd
            def _(pool):
                pool.wait_ge(v, 4)
                nc.gpsimd.tensor_tensor(r[:], m[:], half[:], ALU.pow).then_inc(q, 1)

            @block.scalar
            def _(act):
                act.wait_ge(v, 8)
                tt = t[:].rearrange("p b e -> p (b e)")
                nc.scalar.activation(tt, tt, ACT.Exp, scale=2.0).then_inc(a, 1)

            @block.vector
            def _(dve):
                dve.wait_ge(loaded, 16)
                nc.vector.memset(half[:], -0.5).then_inc(v, 1)
                nc.vector.tensor_tensor(t[:], LG[:], LG[:], ALU.mult).then_inc(v, 1)
                dve.wait_ge(v, 2)
                nc.vector.tensor_reduce(m[:], t[:], AX.X, ALU.add).then_inc(v, 1)
                dve.wait_ge(v, 3)
                nc.vector.tensor_scalar(m[:], m[:], 1.0 / NE, 1.1920928955078125e-07, ALU.mult, ALU.add
                                        ).then_inc(v, 1)
                dve.wait_ge(q, 1)
                nc.vector.tensor_tensor(t[:], LG[:], r[:].unsqueeze(2).to_broadcast(wide), ALU.mult).then_inc(v, 1)
                dve.wait_ge(v, 5)
                nc.vector.tensor_tensor(t[:], t[:], rw[:].unsqueeze(1).to_broadcast(wide), ALU.mult).then_inc(v, 1)
                dve.wait_ge(v, 6)
                nc.vector.tensor_reduce(m[:], t[:], AX.X, ALU.max).then_inc(v, 1)
                dve.wait_ge(v, 7)
                nc.vector.tensor_tensor(t[:], t[:], m[:].unsqueeze(2).to_broadcast(wide), ALU.subtract).then_inc(v, 1)
                dve.wait_ge(a, 1)
                nc.vector.tensor_reduce(m[:], t[:], AX.X, ALU.add).then_inc(v, 1)
                dve.wait_ge(v, 9)
                nc.vector.reciprocal(m[:], m[:]).then_inc(v, 1)
                dve.wait_ge(v, 10)
                nc.vector.tensor_scalar(r[:], m[:], 1e-6, None, ALU.add).then_inc(v, 1)
                dve.wait_ge(v, 11)
                nc.vector.reciprocal(r[:], r[:]).then_inc(v, 1)
                dve.wait_ge(v, 12)
                nc.vector.tensor_tensor(scale[:], m[:], r[:], ALU.mult).then_inc(v, 1)
                dve.wait_ge(v, 13)


def top2_weights(nc, LG, WT, rank_in):
    tag = "T_"
    with ExitStack() as ctx:
        def sb(name, shape):
            return ctx.enter_context(nc.sbuf_tensor(tag + name, shape, F32))

        rank = sb("rank", [P, NE])
        l2 = sb("l2", [P, NB, NE])
        e = [sb(f"e{i}", [P, NB, NE]) for i in range(2)]
        m = [sb(f"m{i}", [P, NB]) for i in range(2)]
        k = sb("k", [P, NB])
        d = sb("d", [P, NB])
        loaded = ctx.enter_context(nc.semaphore(tag + "loaded"))
        v = ctx.enter_context(nc.semaphore(tag + "v"))
        a = ctx.enter_context(nc.semaphore(tag + "a"))
        wide = [P, NB, NE]

        with nc.Block() as block:
            @block.sync
            def _(sp):
                sp.dma_start(rank[:], rank_in.partition_broadcast(P)).then_inc(loaded, 16)

            @block.scalar
            def _(act):
                act.wait_ge(v, 12)
                nc.scalar.activation(d[:], d[:], ACT.Exp).then_inc(a, 1)

            @block.vector
            def _(dve):
                dve.wait_ge(loaded, 16)

                def b(x):
                    return x[:].unsqueeze(2).to_broadcast(wide)

                n = 0
                for i, src in ((0, LG), (1, l2)):
                    nc.vector.tensor_reduce(m[i][:], src[:], AX.X, ALU.max).then_inc(v, 1)
                    dve.wait_ge(v, n + 1)
                    nc.vector.tensor_tensor(e[i][:], src[:], b(m[i]), ALU.is_equal).then_inc(v, 1)
                    dve.wait_ge(v, n + 2)
                    nc.vector.tensor_tensor(e[i][:], e[i][:], rank[:].unsqueeze(1).to_broadcast(wide),
                                            ALU.mult).then_inc(v, 1)
                    dve.wait_ge(v, n + 3)
                    nc.vector.tensor_reduce(k[:], e[i][:], AX.X, ALU.max).then_inc(v, 1)
                    dve.wait_ge(v, n + 4)
                    nc.vector.tensor_tensor(e[i][:], e[i][:], b(k), ALU.is_equal).then_inc(v, 1)
                    dve.wait_ge(v, n + 5)
                    n += 5
                    if i == 0:
                        nc.vector.scalar_tensor_tensor(l2[:], e[0][:], MASKED, LG[:], ALU.mult,
                                                       ALU.add).then_inc(v, 1)
                        dve.wait_ge(v, n + 1)
                        n += 1
                nc.vector.tensor_tensor(d[:], m[1][:], m[0][:], ALU.subtract).then_inc(v, 1)
                dve.wait_ge(a, 1)
                nc.vector.tensor_scalar(k[:], d[:], 1.0, None, ALU.add).then_inc(v, 1)
                dve.wait_ge(v, n + 2)
                nc.vector.reciprocal(m[0][:], k[:]).then_inc(v, 1)
                dve.wait_ge(v, n + 3)
                nc.vector.tensor_tensor(m[1][:], d[:], m[0][:], ALU.mult).then_inc(v, 1)
                dve.wait_ge(v, n + 4)
                for i in range(2):
                    nc.vector.tensor_tensor(e[i][:], e[i][:], b(m[i]), ALU.mult).then_inc(v, 1)
                dve.wait_ge(v, n + 6)
                nc.vector.tensor_tensor(WT[:], e[0][:], e[1][:], ALU.add).then_inc(v, 1)
                dve.wait_ge(v, n + 7)


def dense_experts(nc, const, X, XT, scale, w1, b1, w2, b2):
    H = 256
    NC = NE * H // P
    BT = 512
    tag = "E0_"
    with ExitStack() as ctx:
        def sb(name, shape, dt):
            return ctx.enter_context(nc.sbuf_tensor(tag + name, shape, dt))

        def sem(name):
            return ctx.enter_context(nc.semaphore(tag + name))

        U = ctx.enter_context(nc.psum_tensor(tag + "U", [P, 4, 512], F32))
        Y = ctx.enter_context(nc.psum_tensor(tag + "Y", [P, 2, 512], F32))
        T = ctx.enter_context(nc.psum_tensor(tag + "T", [P, 2, 512], F32))
        raw = sb("raw", [P, 2, NC * P], F32)
        W1 = [sb(f"W1{i}", [P, NC * P], F32R) for i in range(2)]
        W2 = [sb(f"W2{i}", [P, NC * P], F32R) for i in range(2)]
        B1 = sb("B1", [P, NC], F32)
        B2 = sb("B2", [P, NE], F32)
        b2sum = sb("b2sum", [P, 1], F32)
        G = sb("G", [P, 4, BT], F32)
        GP = [sb(f"GP{i}", [P, 4, BT], F32R) for i in range(2)]
        yT = sb("yT", [P, 2, BT], F32)
        w_loaded = sem("w_loaded")
        prepared = sem("prepared")
        u_full = sem("u_full")
        g_done = sem("g_done")
        h_done = sem("h_done")
        l_done = sem("l_done")
        d_done = sem("d_done")
        y_done = sem("y_done")
        t_full = sem("t_full")
        x_done = sem("x_done")

        def walk(eng, do):
            def pair(h, last):
                for par in range(2):
                    blk = 2 * h + par
                    for c in range(NC):
                        n = blk * NC + c
                        ahead = c + 2 >= NC
                        if not (last and par == 1 and ahead):
                            do.up(n + 2, (c + 2) % NC, blk + 1 if ahead else blk)
                        do.down(n, c, par, blk)
                        if c == 3 and not (isinstance(blk, int) and blk == 0):
                            do.finish(blk - 1, 1 - par)

            do.up(0, 0, 0)
            do.up(1, 1, 0)
            pair(0, False)
            with eng.Fori(1, NG // 2 - 1) as h:
                pair(h, False)
            pair(NG // 2 - 1, True)
            do.finish(NG - 1, 1)

        with nc.Block() as block:
            @block.sync
            def _(sp):
                sp.dma_start(raw[:, 0, :].rearrange("p (e h) -> p e h", e=NE),
                             w1.rearrange("e d h -> d e h")).then_inc(w_loaded, 16)
                sp.dma_start(raw[:, 1, :].rearrange("p (c d) -> p c d", c=NC),
                             w2.rearrange("e (c p) d -> p (e c) d", p=P)).then_inc(w_loaded, 16)
                sp.dma_start(B1[:], b1).then_inc(w_loaded, 16)
                sp.dma_start(B2[:], b2).then_inc(w_loaded, 16)

            @block.vector
            def _(dve):
                dve.wait_ge(w_loaded, 64)
                at = split(nc, W1[0][:], W1[1][:], raw[:, 0, :], prepared, 0)
                at = split(nc, W2[0][:], W2[1][:], raw[:, 1, :], prepared, at)
                nc.vector.tensor_reduce(b2sum[:], B2[:], AX.X, ALU.add).then_inc(prepared, 1)

                class do:
                    up = staticmethod(lambda *a: None)

                    @staticmethod
                    def down(n, c, par, blk):
                        dve.wait_ge(g_done, n + 1)
                        need(dve, d_done, n - 3)
                        nc.vector.tensor_copy(GP[0][:, c % 4, :], G[:, c % 4, :]).then_inc(h_done, 1)
                        dve.wait_ge(h_done, n + 1)
                        nc.vector.tensor_tensor(GP[1][:, c % 4, :], G[:, c % 4, :],
                                                GP[0][:, c % 4, :].bitcast(F32), ALU.subtract).then_inc(l_done, 1)

                    @staticmethod
                    def finish(blk, par):
                        dve.wait_ge(t_full, blk + 1)
                        for j in range(GB):
                            t = blk * GB + j
                            nc.vector.scalar_tensor_tensor(X[:, t, :], T[:, par, j * P:(j + 1) * P],
                                                           scale[:, bass.ds(t, 1)], X[:, t, :], ALU.mult,
                                                           ALU.add).then_inc(x_done, 1)

                walk(dve, do)
                dve.wait_ge(x_done, NB)

            @block.scalar
            def _(act):
                class do:
                    up = staticmethod(lambda *a: None)

                    @staticmethod
                    def down(n, c, par, blk):
                        act.wait_ge(u_full, n + 1)
                        need(act, l_done, n - 3)
                        nc.scalar.activation(G[:, c % 4, :], U[:, c % 4, :], ACT.Gelu, bias=B1[:, c:c + 1]
                                             ).then_inc(g_done, 1)
                        if c == 2:
                            self_finish(blk - 1, 1 - par)

                    finish = staticmethod(lambda *a: None)

                def self_finish(blk, par):
                    if isinstance(blk, int) and blk < 0:
                        return
                    act.wait_ge(d_done, (blk + 1) * NC)
                    nc.scalar.activation(yT[:, par, :], Y[:, par, :], ACT.Identity, bias=b2sum[:]
                                         ).then_inc(y_done, 1)

                act.wait_ge(prepared, 5)
                walk(act, do)
                self_finish(NG - 1, 1)

            @block.tensor
            def _(pe):
                class do:
                    @staticmethod
                    def up(n, c, blk):
                        need(pe, g_done, n - 3)
                        passes(nc, U[:, c % 4, :], [W[:, c * P:(c + 1) * P] for W in W1],
                               [x[:, bass.ds(blk * BT, BT)] for x in XT]).then_inc(u_full, 1)

                    @staticmethod
                    def down(n, c, par, blk):
                        pe.wait_ge(l_done, n + 1)
                        if c == 0:
                            need(pe, y_done, blk - 1)
                        passes(nc, Y[:, par, :], [W[:, c * P:(c + 1) * P] for W in W2],
                               [g[:, c % 4, :] for g in GP], start=c == 0, stop=c == NC - 1).then_inc(d_done, 1)

                    @staticmethod
                    def finish(blk, par):
                        pe.wait_ge(y_done, blk + 1)
                        need(pe, x_done, GB * (blk - 1))
                        for j in range(GB):
                            last = pe.transpose(T[:, par, j * P:(j + 1) * P], yT[:, par, j * P:(j + 1) * P],
                                                const.ident[:])
                        last.then_inc(t_full, 1)

                pe.wait_ge(prepared, 5)
                walk(pe, do)


def routed_experts(nc, const, X, XT, WT, w1, b1, w2, b2, out):
    H = 512
    NC = H // P
    BT = 512
    tag = "E1_"
    with ExitStack() as ctx:
        def sb(name, shape, dt):
            return ctx.enter_context(nc.sbuf_tensor(tag + name, shape, dt))

        def sem(name):
            return ctx.enter_context(nc.semaphore(tag + name))

        U = ctx.enter_context(nc.psum_tensor(tag + "U", [P, 2, 2, 512], F32))
        Y = ctx.enter_context(nc.psum_tensor(tag + "Y", [P, 2, 512], F32))
        T = ctx.enter_context(nc.psum_tensor(tag + "T", [P, 2, 512], F32))
        raw1 = sb("raw1", [P, 2 * H], F32)
        raw2 = sb("raw2", [P, NC, P], F32)
        W1 = [sb(f"W1{i}", [P, 2, 2 * H], F32R) for i in range(2)]
        W2 = [sb(f"W2{i}", [P, 2, H], F32R) for i in range(2)]
        B1 = sb("B1", [P, NE * 2 * NC], F32)
        B2 = sb("B2", [P, NE], F32)
        SL = sb("SL", [P, 2, BT], F32)
        G = sb("G", [P, 2, BT], F32)
        GP = [sb(f"GP{i}", [P, 2, BT], F32R) for i in range(2)]
        yT = sb("yT", [P, 2, BT], F32)
        b_loaded = sem("b_loaded")
        w_loaded = [sem(f"w_loaded{i}") for i in range(2)]
        w_split = sem("w_split")
        u_full = sem("u_full")
        s_done = sem("s_done")
        g_done = sem("g_done")
        h_done = sem("h_done")
        l_done = sem("l_done")
        d_done = sem("d_done")
        y_done = sem("y_done")
        t_full = sem("t_full")
        x_done = sem("x_done")
        stored = sem("stored")

        def walk(eng, do):
            def blocks(e, ep, h, first, last, final):
                for par in range(2):
                    blk = 2 * h + par
                    m = e * NG + blk
                    for c in range(NC):
                        n = m * NC + c
                        if c < NC - 1:
                            do.up(n + 1, (c + 1) % 2, c + 1, blk, e, ep)
                        elif par == 0 or not last:
                            do.up(n + 1, 0, 0, blk + 1, e, ep)
                        elif not final:
                            do.next_weights(e + 1, 1 - ep)
                            do.up(n + 1, 0, 0, 0, e + 1, 1 - ep)
                        do.down(n, c, par, m, e, ep)
                        if c == 1 and not (first and par == 0):
                            if par == 1 or not (isinstance(h, int) and h == 0):
                                do.finish(m - 1, 1 - par, blk - 1, e)
                            else:
                                do.finish(m - 1, 1 - par, NG - 1, e - 1)

            def expert(e, ep, first, final):
                if not final:
                    do.load(e + 1, 1 - ep)
                blocks(e, ep, 0, first, False, False)
                with eng.Fori(1, NG // 2 - 1) as h:
                    blocks(e, ep, h, False, False, False)
                blocks(e, ep, NG // 2 - 1, False, True, final)

            do.load(0, 0)
            do.next_weights(0, 0)
            do.up(0, 0, 0, 0, 0, 0)
            expert(0, 0, True, False)
            expert(1, 1, False, False)
            with eng.Fori(1, NE // 2 - 1) as eh:
                expert(2 * eh, 0, False, False)
                expert(2 * eh + 1, 1, False, False)
            expert(NE - 2, 0, False, False)
            expert(NE - 1, 1, False, True)
            do.finish(NE * NG - 1, 1, NG - 1, NE - 1)

        def nothing(*a):
            return None

        with nc.Block() as block:
            @block.sync
            def _(sp):
                sp.dma_start(B1[:], b1).then_inc(b_loaded, 16)
                sp.dma_start(B2[:], b2).then_inc(b_loaded, 16)
                for e in range(NE):
                    if e:
                        sp.wait_ge(w_split, 4 * e)
                    sp.dma_start(raw1[:], w1[e]).then_inc(w_loaded[e % 2], 16)
                    sp.dma_start(raw2[:], w2[e].rearrange("(c p) d -> p c d", p=P)).then_inc(w_loaded[e % 2], 16)
                with sp.Fori(0, NG) as g:
                    sp.wait_ge(x_done, (NE - 1) * NB + GB * (g + 1))
                    sp.dma_start(out[bass.ds(g * GB, GB)].rearrange("b s d -> s b d"),
                                 X[:, bass.ds(g * GB, GB), :]).then_inc(stored, 16)
                sp.wait_ge(stored, 16 * NG)

            @block.vector
            def _(dve):
                class do:
                    up = load = staticmethod(nothing)

                    @staticmethod
                    def next_weights(e, ep):
                        pair = (e - ep) // 2 if isinstance(e, int) else None
                        dve.wait_ge(w_loaded[ep], 32 * pair + 32 if pair is not None else 16 * (e - ep) + 32)
                        for i, (W, r) in enumerate(((W1, raw1[:]), (W2, raw2[:].rearrange("p c d -> p (c d)")))):
                            nc.vector.tensor_copy(W[0][:, ep, :], r).then_inc(w_split, 1)
                            dve.wait_ge(w_split, 4 * e + 2 * i + 1)
                            nc.vector.tensor_tensor(W[1][:, ep, :], r, W[0][:, ep, :].bitcast(F32),
                                                    ALU.subtract).then_inc(w_split, 1)

                    @staticmethod
                    def down(n, c, par, m, e, ep):
                        dve.wait_ge(s_done, n + 1)
                        bias = B1[:, bass.ds(e * 2 * NC + NC + c, 1)]
                        nc.vector.scalar_tensor_tensor(G[:, c % 2, :], U[:, c % 2, 1, :], bias, SL[:, c % 2, :],
                                                       ALU.add, ALU.mult).then_inc(g_done, 1)
                        dve.wait_ge(h_done, n + 1)
                        nc.vector.tensor_tensor(GP[1][:, c % 2, :], G[:, c % 2, :],
                                                GP[0][:, c % 2, :].bitcast(F32), ALU.subtract).then_inc(l_done, 1)

                    @staticmethod
                    def finish(m, par, blk, e):
                        dve.wait_ge(t_full, m + 1)
                        need(dve, x_done, GB * m)
                        for j in range(GB):
                            t = blk * GB + j
                            nc.vector.scalar_tensor_tensor(X[:, t, :], T[:, par, j * P:(j + 1) * P],
                                                           WT[:, t, bass.ds(e, 1)], X[:, t, :], ALU.mult,
                                                           ALU.add).then_inc(x_done, 1)

                dve.wait_ge(b_loaded, 32)
                walk(dve, do)

            @block.scalar
            def _(act):
                class do:
                    up = load = next_weights = staticmethod(nothing)

                    @staticmethod
                    def down(n, c, par, m, e, ep):
                        act.wait_ge(u_full, n + 1)
                        wait_apart(act, const, g_done, n - 1)
                        nc.scalar.activation(SL[:, c % 2, :], U[:, c % 2, 0, :], ACT.Silu,
                                             bias=B1[:, bass.ds(e * 2 * NC + c, 1)]).then_inc(s_done, 1)
                        act.wait_ge(g_done, n + 1)
                        need(act, d_done, n - 1)
                        nc.scalar.copy(GP[0][:, c % 2, :], G[:, c % 2, :]).then_inc(h_done, 1)

                    @staticmethod
                    def finish(m, par, blk, e):
                        wait_apart(act, const, d_done, (m + 1) * NC)
                        nc.scalar.activation(yT[:, par, :], Y[:, par, :], ACT.Identity,
                                             bias=B2[:, bass.ds(e, 1)]).then_inc(y_done, 1)

                act.wait_ge(b_loaded, 32)
                walk(act, do)

            @block.tensor
            def _(pe):
                class do:
                    load = staticmethod(nothing)

                    @staticmethod
                    def next_weights(e, ep):
                        pe.wait_ge(w_split, 4 * (e + 1))

                    @staticmethod
                    def up(n, slot, c, blk, e, ep):
                        need(pe, g_done, n - 1)
                        for half in range(2):
                            w = [W[:, ep, half * H + c * P:half * H + (c + 1) * P] for W in W1]
                            last = passes(nc, U[:, slot, half, :], w, [x[:, bass.ds(blk * BT, BT)] for x in XT])
                        last.then_inc(u_full, 1)

                    @staticmethod
                    def down(n, c, par, m, e, ep):
                        pe.wait_ge(l_done, n + 1)
                        if c == 0:
                            need(pe, y_done, m - 1)
                        passes(nc, Y[:, par, :], [W[:, ep, c * P:(c + 1) * P] for W in W2],
                               [g[:, c % 2, :] for g in GP], start=c == 0, stop=c == NC - 1).then_inc(d_done, 1)

                    @staticmethod
                    def finish(m, par, blk, e):
                        pe.wait_ge(y_done, m + 1)
                        need(pe, x_done, GB * (m - 1))
                        for j in range(GB):
                            last = pe.transpose(T[:, par, j * P:(j + 1) * P], yT[:, par, j * P:(j + 1) * P],
                                                const.ident[:])
                        last.then_inc(t_full, 1)

                walk(pe, do)


def build(nc, a, out):
    with ExitStack() as ctx:
        X = ctx.enter_context(nc.sbuf_tensor("X", [P, NB, P], F32))
        const = Constants(nc, ctx, a["identity"])
        for layer in range(2):
            w = f"L{layer}_xattn_"
            attention(nc, const, X, layer, a["x"] if layer == 0 else None, a["ctx_1024"],
                      a["mask_BxSxS2_bk1"], a[w + "Wq"], a[w + "Wk"], a[w + "Wv"], a[w + "Wo"],
                      a[w + "bo"], a["signs"])
            with ExitStack() as ffn:
                XT = [ffn.enter_context(nc.sbuf_tensor(f"XT{layer}{i}", [P, NB * P], F32R)) for i in range(2)]
                LG = ffn.enter_context(nc.sbuf_tensor(f"LG{layer}", [P, NB, NE], F32))
                if layer == 0:
                    normalise_all(nc, const, X, 0, XT, LG, a["L0_ffn_gate_w"], a["L0_ffn_gate_b"])
                    scale = ffn.enter_context(nc.sbuf_tensor("scale", [P, NB], F32))
                    gate_scale(nc, LG, scale, a["L0_ffn_rms_w"])
                    dense_experts(nc, const, X, XT, scale, a["L0_ffn_w1"], a["L0_ffn_b1"], a["L0_ffn_w2"],
                                  a["L0_ffn_b2"])
                else:
                    normalise_all(nc, const, X, 1, XT, LG, a["L1_ffn_router_w"], a["L1_ffn_router_b"])
                    WT = ffn.enter_context(nc.sbuf_tensor("WT", [P, NB, NE], F32))
                    top2_weights(nc, LG, WT, a["rank"])
                    routed_experts(nc, const, X, XT, WT, a["L1_ffn_w1"], a["L1_ffn_b1"], a["L1_ffn_w2"],
                                   a["L1_ffn_b2"], out)


def kernel(**inputs):
    import numpy as np
    import concourse.bacc as bacc
    from concourse.bass_utils import run_bass_kernel_spmd

    def turned(a, *order):
        return np.ascontiguousarray(np.transpose(a, order))

    a = {k: np.asarray(v) for k, v in inputs.items()}
    for name in ("Wq", "Wk", "Wv", "Wo"):
        a[f"L0_xattn_{name}"] = turned(a[f"L0_xattn_{name}"], 1, 0)
    a["L0_ffn_gate_w"] = turned(a["L0_ffn_gate_w"], 1, 0)
    a["L1_ffn_router_w"] = turned(a["L1_ffn_router_w"], 1, 0)
    a["L1_ffn_w1"] = turned(a["L1_ffn_w1"], 0, 2, 1)
    a["L1_ffn_w2"] = turned(a["L1_ffn_w2"], 0, 2, 1)
    for layer in range(2):
        b1 = a[f"L{layer}_ffn_b1"]
        a[f"L{layer}_ffn_b1"] = turned(b1.reshape(-1, P), 1, 0)
        a[f"L{layer}_ffn_b2"] = turned(a[f"L{layer}_ffn_b2"], 1, 0)
    row = np.arange(P) % 32 // 8
    a["identity"] = np.eye(P, dtype=np.float32)
    a["signs"] = np.stack([row >= 2, row % 2 == 1], 1).astype(np.float32)
    a["rank"] = np.arange(NE, 0, -1, dtype=np.float32)
    a = {k: np.ascontiguousarray(v) for k, v in a.items()}

    nc = bacc.Bacc("TRN2", target_bir_lowering=False, num_devices=1)
    aps = {k: nc.dram_tensor(k, v.shape, mybir.dt.from_np(v.dtype), kind="ExternalInput").ap() for k, v in a.items()}
    out = nc.dram_tensor("out", (NB, P, P), F32, kind="ExternalOutput").ap()
    build(nc, aps, out)
    r = run_bass_kernel_spmd(nc, [a], core_ids=[0])
    return r.results[0]["out"]
```

```python
from contextlib import ExitStack

import concourse.bass as bass
from concourse import mybir

F32 = mybir.dt.float32
F32R = mybir.dt.float32r
BF16 = mybir.dt.bfloat16
U8 = mybir.dt.uint8
ALU = mybir.AluOpType
ACT = mybir.ActivationFunctionType
AX = mybir.AxisListType

P = 128
NB = 64
KL = 77
NH = 16
GB = 4
NG = NB // GB
UH = 8
UPG = 2 * GB
EPS = 1e-5
NE = 8
RB = 4
MASKED = -3.3895313892515355e38


def need(eng, sem, value):
    if not (isinstance(value, int) and value <= 0):
        eng.wait_ge(sem, value)


def split(nc, hi, lo, full, sem, at):
    nc.vector.tensor_copy(hi, full).then_inc(sem, 1)
    nc.vector.wait_ge(sem, at + 1)
    nc.vector.tensor_tensor(lo, full, hi.bitcast(F32), ALU.subtract).then_inc(sem, 1)
    return at + 2


def passes(nc, out, left, right, start=True, stop=True):
    nc.tensor.matmul(out, left[0], right[0], start=start, stop=False)
    nc.tensor.matmul(out, left[0], right[1], start=False, stop=False)
    return nc.tensor.matmul(out, left[1], right[0], start=False, stop=stop)


class Constants:

    def __init__(self, nc, ctx, ident_in):
        def sb(name, shape, dt):
            return ctx.enter_context(nc.sbuf_tensor(name, shape, dt))

        self.ident = sb("ident", [P, P], F32)
        self.ident_bf = sb("ident_bf", [P, P], BF16)
        self.minus_half = sb("minus_half", [P, NB], F32)
        ident_loaded = ctx.enter_context(nc.semaphore("ident_loaded"))
        const_made = ctx.enter_context(nc.semaphore("const_made"))
        self.passed = ctx.enter_context(nc.semaphore("passed"))
        with nc.Block() as block:
            @block.sync
            def _(sp):
                sp.dma_start(self.ident[:], ident_in).then_inc(ident_loaded, 16)
                sp.wait_ge(ident_loaded, 16)

            @block.vector
            def _(dve):
                nc.vector.memset(self.minus_half[:], -0.5).then_inc(const_made, 1)
                dve.wait_ge(ident_loaded, 16)
                nc.vector.tensor_copy(self.ident_bf[:], self.ident[:]).then_inc(const_made, 1)
                dve.wait_ge(const_made, 2)


def wait_apart(eng, const, sem, value):
    need(eng, sem, value)
    if not isinstance(value, int):
        eng.sem_inc(const.passed, 1)


class Norm:

    def __init__(self, nc, sb, sem, const, X):
        self.nc, self.X, self.const = nc, X, const
        self.stats = sb("stats", [P, GB, 6], F32)
        self.mv = sb("mv", [P, GB, 2], F32)
        self.ve = sb("ve", [P, GB], F32)
        self.rstd = sb("rstd", [P, GB], F32)
        self.xn = sb("xn", [P, GB, P], F32)
        self.step = sem("ln_step")
        self.rstd_done = sem("rstd_done")
        self.xn_done = sem("xn_done")

    def statistics(self, dve, g):
        nc, n = self.nc, g * (2 * GB + 1)
        for j in range(GB):
            nc.vector.bn_stats(self.stats[:, j, :], self.X[:, g * GB + j, :]).then_inc(self.step, 1)
        for j in range(GB):
            wait_apart(dve, self.const, self.step, n + j + 1)
            nc.vector.bn_aggr(self.mv[:, j, :], self.stats[:, j, :]).then_inc(self.step, 1)
        dve.wait_ge(self.step, n + 2 * GB)
        nc.vector.tensor_scalar(self.ve[:], self.mv[:, :, 1], EPS, None, ALU.add).then_inc(self.step, 1)

    def scaling(self, dve, g):
        dve.wait_ge(self.rstd_done, g + 1)
        for j in range(GB):
            self.nc.vector.tensor_scalar(self.xn[:, j, :], self.X[:, g * GB + j, :], self.mv[:, j, 0:1],
                                    self.rstd[:, j:j + 1], ALU.subtract, ALU.mult).then_inc(self.xn_done, 1)

    def on_pool(self, pool, g):
        pool.wait_ge(self.step, (g + 1) * (2 * GB + 1))
        self.nc.gpsimd.tensor_tensor(self.rstd[:], self.ve[:], self.const.minus_half[:, 0:GB],
                                     ALU.pow).then_inc(self.rstd_done, 1)


def attention(nc, const, X, MV, layer, x_in, ctx_in, mask_in, wq, wk, wv, wo, bo, signs):
    small = layer == 0
    DH = 8 if small else 64
    INNER = NH * DH
    SCALE = float(DH) ** -0.5
    VW = DH + 1
    QC = 4 if small else 8
    KW = GB * KL
    KBW = 4 * KL if small else 2 * KL
    CPB = 1 if small else 2
    NV = 1 if small else 2 * GB
    OC = INNER // P
    OH = 8 if small else 4
    SQ = 4 if small else 2
    tag = f"L{layer}_"

    FRONT = [("xt", 0), ("ct", 0)] + [("k", c) for c in range(QC)] + [("q", c) for c in range(QC)] \
        + [("v", c) for c in range(NV)]

    def front_of(step):
        if step == UPG - 1:
            return FRONT[:2]
        later = len(FRONT) - 2
        return FRONT[2 + step * later // (UPG - 1):2 + (step + 1) * later // (UPG - 1)]

    def place(step):
        return (step // 2, step % 2) if small else (2 * (step // 4) + step % 2, step // 2 % 2)

    def tail_of(t):
        if small:
            return {10: [("ot", 0)], 11: [("y", 0)], 12: [("yt", 0)]}.get(t, [])
        jobs = [("y", (t - 3) // 2)] if t in (3, 5, 7, 9) else []
        jobs += [("yt", (t - 6) // 4)] if t in (6, 10) else []
        return jobs + ([("ot", t - 1)] if 1 <= t <= UPG else [])

    TAIL = sum(len(tail_of(t)) for t in range(2 * UPG))
    BODY = 2 * (len(FRONT) + UPG * (UH // OH) + TAIL)
    assert BODY % RB == 0

    with ExitStack() as ctx:
        def sb(name, shape, dt):
            return ctx.enter_context(nc.sbuf_tensor(tag + name, shape, dt))

        def sem(name):
            return ctx.enter_context(nc.semaphore(tag + name))

        S = ctx.enter_context(nc.psum_tensor(tag + "S", [P, 2, 512], F32))
        PT = ctx.enter_context(nc.psum_tensor(tag + "PT", [P, 2, 512], F32))
        R = ctx.enter_context(nc.psum_tensor(tag + "R", [P, RB, 512], F32))

        WQ = [sb(f"WQ{i}", [P, QC * P], F32R) for i in range(2)]
        WK = [sb(f"WK{i}", [P, QC * P], F32R) for i in range(2)]
        WV = [sb(f"WV{i}", [P, INNER], F32R) for i in range(2)]
        WO = [sb(f"WO{i}", [P, OC * P], F32R) for i in range(2)]
        bo_col = sb("bo_col", [P, 1], F32)
        norm = Norm(nc, sb, sem, const, X)
        cx = sb("cx", [KL, GB, P], F32)
        xT = [sb(f"xT{i}", [P, GB * P], F32R) for i in range(2)]
        cT = [sb(f"cT{i}", [P, KW], F32R) for i in range(2)]
        QD = F32R if small else F32
        qT = sb("qT", [P, 2, QC, GB * P], QD)
        kbd = sb("kbd", [P, 2, QC, GB, KBW], QD)
        Sm = sb("Sm", [P, 2, UH, KL], F32)
        if small:
            sgn = sb("sgn", [P, 2], F32)
            rounded = sb("rounded", [P, RB, GB * P], F32R)
            kst = sb("kst", [P, QC, KW], F32R)
            raw = Sm[:].rearrange("p a h k -> p (a h k)")
        else:
            mk = sb("mk", [P, 2, GB, KL], U8)
            mb = sb("mb", [P, 2, GB, KL], BF16)
            raw = kbd[:].rearrange("p a c b k -> p (a c b k)")
        V = sb("V", [KL, 2, GB, NH, VW], F32)
        nmax = sb("nmax", [P, 2, UH], F32)
        PTs = sb("PTs", [KL, 2, 2, 512], F32)
        rden = sb("rden", [P, 2, OH], F32)
        O = sb("O", [P, 2, GB, NH, DH] if small else [P, 2, UH, DH], F32)
        OT = [sb(f"OT{i}", [P, max(1, OC // 2), SQ * P], F32R) for i in range(2)]
        yT = sb("yT", [P, SQ * P], F32)
        st_new = sb("st_new", [P, GB, 6], F32)
        mv_new = sb("mv_new", [P, GB, 2], F32)

        w_loaded = sem("w_loaded")
        prepared = sem("prepared")
        ready = sem("ready")
        x_loaded = [sem(f"x_loaded{i}") for i in range(2)]
        ctx_loaded = sem("ctx_loaded")
        mask_loaded = [sem(f"mask_loaded{i}") for i in range(2)]
        ring_full = [sem(f"ring_full{i}") for i in range(RB)]
        ring_done = [sem(f"ring_done{i}") for i in range(RB)]
        xt_hi = sem("xt_hi")
        ct_hi = sem("ct_hi")
        qk_hi = sem("qk_hi")
        kbd_done = sem("kbd_done")
        mask_done = sem("mask_done")
        s_full = sem("s_full")
        max_done = sem("max_done")
        sub_done = sem("sub_done")
        exp_done = sem("exp_done")
        pt_full = sem("pt_full")
        pt_done = sem("pt_done")
        rec_done = sem("rec_done")
        ot_hi = sem("ot_hi")
        x_done = sem("x_done")
        new_stats = sem("new_stats")
        mv_done = sem("mv_done")

        Vrows = V[:].rearrange("p a b h w -> p a (b h) w")

        ring_base = [0]

        def walk(eng, do, exp_after_transposes=False):
            job = [0]
            ring_base[0] = 0

            def take():
                job[0] += 1
                return (job[0] - 1) % RB, ring_base[0] + (job[0] - 1) // RB, job[0] - 1

            def tail(t, g, par):
                for kind, c in tail_of(t):
                    do.tail(kind, c, g, par, take())

            def pair(h, first, last):
                for par in range(2):
                    for st in range(UPG):
                        g, u = 2 * h + par, (2 * h + par) * UPG + st
                        final = last and par == 1
                        nst, npar = (st + 1) % UPG, (par + (st + 1) // UPG) % 2
                        more = not (final and st == UPG - 1)
                        if more and not exp_after_transposes:
                            do.scores(u + 1, nst, npar, g + 1 if nst == 0 else g)
                        do.transposes(u, st)
                        if more and exp_after_transposes:
                            do.scores(u + 1, nst, npar, g + 1 if nst == 0 else g)
                        if st < UPG - 1 and not final:
                            for kind, c in front_of(st):
                                do.front(kind, c, g + 1, 1 - par, h + par, take())
                        if st == UPG - 1 and not last:
                            for kind, c in front_of(st):
                                do.front(kind, c, g + 2, par, h + 1, take())
                        if not (first and par == 0):
                            tail(st + UPG, g - 1, 1 - par)
                        tail(st, g, par)
                        if not small:
                            for cc in range(UH // OH):
                                do.values(u, st, par, cc, take())
                        elif not (first and par == 0 and st == 0):
                            for cc in range(UH // OH):
                                do.values(u - 1, (st - 1) % UPG, par if st else 1 - par, cc, take())
                        if st == 4 and not last:
                            do.norm(g + 2, par, h + 1)
                        if st == UPG - 2 and not last:
                            do.scaling(g + 2)

            do.norm(0, 0, 0)
            do.scaling(0)
            for kind, c in FRONT:
                do.front(kind, c, 0, 0, 0, take())
            do.scores(0, 0, 0, 0)
            do.norm(1, 1, 0)
            do.scaling(1)
            for kind, c in FRONT[:2]:
                do.front(kind, c, 1, 1, 0, take())
            pair(0, True, False)
            with eng.Fori(1, NG // 2 - 1) as h:
                ring_base[0] = (h - 1) * (BODY // RB)
                pair(h, False, False)
            ring_base[0] = (NG // 2 - 3) * (BODY // RB)
            pair(NG // 2 - 1, False, True)
            for t in range(UPG, 2 * UPG):
                tail(t, NG - 1, 1)
                if t == UPG and small:
                    for cc in range(UH // OH):
                        do.values(NG * UPG - 1, UPG - 1, 1, cc, take())

        YT = sum(kind == "yt" for t in range(2 * UPG) for kind, _ in tail_of(t))
        OTJ = sum(kind == "ot" for t in range(2 * UPG) for kind, _ in tail_of(t))

        def ot_job(bank):
            return R[:, bank, :].rearrange("p (c t) -> p c t", t=P)

        def ot_slot(part, c):
            if small:
                return part[:, 0, :].rearrange("p (c t) -> p c t", t=P)
            return part[:, :, (c % 2) * P:(c % 2 + 1) * P]

        def zero_keys(engine, par):
            engine.memset(kbd[:, par].rearrange("p c b k -> p (c b k)").bitcast(F32), 0.0).then_inc(ready, 1)

        with nc.Block() as block:
            @block.sync
            def _(sp):
                for t, w in enumerate((wq, wk, wv, wo)):
                    dst = raw[:, t * INNER:(t + 1) * INNER]
                    if t == 3 and not small:
                        dst = dst.rearrange("p (c d) -> p c d", c=OC)
                        w = w.rearrange("(c p) d -> p c d", p=P)
                    sp.dma_start(dst, w).then_inc(w_loaded, 16)
                sp.dma_start(bo_col[:], bo.unsqueeze(1)).then_inc(w_loaded, 16)
                if small:
                    sp.dma_start(sgn[:], signs).then_inc(w_loaded, 16)

                def load(g, par):
                    if x_in is not None:
                        sp.dma_start(X[:, bass.ds(g * GB, GB), :],
                                     x_in[bass.ds(g * GB, GB)].rearrange("b s d -> s b d")
                                     ).then_inc(x_loaded[par], 16)
                    if not small:
                        wait_apart(sp, const, mask_done, g - 1)
                        sp.dma_start(mk[:, par], mask_in[bass.ds(g * GB, GB)].rearrange("b s k -> s b k")
                                     ).then_inc(mask_loaded[par], 16)
                    wait_apart(sp, const, ct_hi, g)
                    sp.dma_start(cx[:], ctx_in[bass.ds(g * GB, GB)].rearrange("b k d -> k b d")
                                 ).then_inc(ctx_loaded, 16)

                load(0, 0)
                load(1, 1)
                with sp.Fori(1, NG // 2) as h:
                    for par in range(2):
                        load(2 * h + par, par)

            @block.gpsimd
            def _(pool):
                class do:
                    @staticmethod
                    def front(kind, c, g, par, h, job):
                        bank, n, _ = job
                        if kind == "ct" and not small:
                            pool.wait_ge(mask_loaded[par], 16 * h + 16)
                            wait_apart(pool, const, s_full, UPG * (g - 1))
                            nc.gpsimd.tensor_scalar(mb[:, par], mk[:, par], MASKED, None,
                                                    ALU.mult).then_inc(mask_done, 1)
                        if kind == "k" and small:
                            wait_apart(pool, const, ring_done[bank], n + 1)
                            for r in range(4):
                                rows = slice(32 * r, 32 * r + 32)
                                nc.gpsimd.tensor_copy(
                                    kbd[rows, par, c, :, r * KL:(r + 1) * KL],
                                    kst[rows, c, :].rearrange("p (b k) -> p b k", b=GB)).then_inc(kbd_done, 1)

                    @staticmethod
                    def norm(g, par, h):
                        if small:
                            need(pool, kbd_done, 4 * QC * g)
                        norm.on_pool(pool, g)

                    scaling = scores = transposes = values = tail = staticmethod(lambda *a: None)

                zero_keys(nc.gpsimd, 1)
                pool.wait_ge(ready, 3)
                walk(pool, do)

            @block.scalar
            def _(act):
                class do:
                    @staticmethod
                    def front(kind, c, g, par, h, job):
                        bank, n, _ = job
                        if kind == "q" and not small:
                            return
                        act.wait_ge(ring_full[bank], n + 1)
                        if kind == "xt":
                            nc.scalar.copy(xT[0][:], R[:, bank, :]).then_inc(xt_hi, 1)
                        elif kind == "ct":
                            nc.scalar.copy(cT[0][:], R[:, bank, 0:KW]).then_inc(ct_hi, 1)
                        elif kind == "q":
                            nc.scalar.copy(rounded[:, bank, :], R[:, bank, :]).then_inc(qk_hi, 1)
                        elif kind == "k" and small:
                            nc.scalar.copy(rounded[:, bank, 0:KW], R[:, bank, 0:KW]).then_inc(qk_hi, 1)
                        elif kind == "k":
                            for r in range(2):
                                rows = slice(64 * r, 64 * r + 64)
                                last = nc.scalar.copy(kbd[rows, par, c, :, r * KL:(r + 1) * KL],
                                                      R[rows, bank, 0:KW].rearrange("p (b k) -> p b k", b=GB))
                            last.then_inc(ring_done[bank], 1)
                        elif small:
                            nc.scalar.copy(Vrows[:, par, :, 0:DH],
                                           R[0:KL, bank, :].rearrange("p (h w) -> p h w", w=DH)
                                           ).then_inc(ring_done[bank], 1)
                        else:
                            nc.scalar.copy(Vrows[:, par, UH * c:UH * (c + 1), 0:DH],
                                           R[0:KL, bank, :].rearrange("p (h w) -> p h w", w=DH)
                                           ).then_inc(ring_done[bank], 1)

                    @staticmethod
                    def scores(u, st, par, g):
                        act.wait_ge(sub_done, u + 1)
                        s = Sm[:, st % 2].rearrange("p h k -> p (h k)")
                        nc.scalar.activation(s, s, ACT.Exp, scale=SCALE).then_inc(exp_done, 1)

                    @staticmethod
                    def transposes(u, st):
                        for cc in range(2):
                            act.wait_ge(pt_full, 2 * u + cc + 1)
                            nc.scalar.copy(PTs[:, st % 2, cc, :], PT[0:KL, cc, :]).then_inc(pt_done, 1)

                    @staticmethod
                    def tail(kind, c, g, par, job):
                        bank, n, _ = job
                        if kind == "yt" or (kind == "y" and c % 2):
                            return
                        act.wait_ge(ring_full[bank], n + 1)
                        if kind == "ot":
                            nc.scalar.copy(ot_slot(OT[0], c), ot_job(bank)).then_inc(ot_hi, 1)
                        else:
                            nc.scalar.activation(yT[:], R[:, bank, 0:SQ * P], ACT.Identity, bias=bo_col[:]
                                                 ).then_inc(ring_done[bank], 1)

                    values = norm = scaling = staticmethod(lambda *a: None)

                act.wait_ge(ready, 3)
                walk(act, do, exp_after_transposes=True)

            @block.vector
            def _(dve):
                if small:
                    zero_keys(nc.vector, 0)
                dve.wait_ge(w_loaded, (6 if small else 5) * 16)
                at = 0
                if small:
                    tmp = qT[:].rearrange("p a c t -> p (a c t)")
                    for W, t, lows in ((WQ, 0, (0, 0, 1, 1)), (WK, 1, (0, 1, 0, 1))):
                        parts = [tmp[:, (2 * t + i) * P:(2 * t + i + 1) * P] for i in range(2)]
                        at = split(nc, parts[0], parts[1], raw[:, t * INNER:(t + 1) * INNER], prepared, at)
                        dve.wait_ge(prepared, at)
                        for i in range(2):
                            for dup in range(4):
                                nc.vector.tensor_scalar(
                                    W[i][:].rearrange("p (h k c) -> p h k c", k=4, c=DH)[:, :, dup, :],
                                    parts[i].bitcast(F32).rearrange("p (h c) -> p h c", c=DH),
                                    -1.0 if lows[dup] else 1.0, None, ALU.mult).then_inc(prepared, 1)
                                at += 1
                    todo = ((WV, 2), (WO, 3))
                else:
                    todo = ((WQ, 0), (WK, 1), (WV, 2), (WO, 3))
                for W, t in todo:
                    at = split(nc, W[0][:], W[1][:], raw[:, t * INNER:(t + 1) * INNER], prepared, at)
                dve.wait_ge(prepared, at)
                if not small:
                    zero_keys(nc.vector, 0)
                nc.vector.memset(V[:].rearrange("p a b h w -> p (a b h) w")[:, :, DH:VW], 1.0).then_inc(ready, 1)
                dve.wait_ge(ready, 3)

                class do:
                    @staticmethod
                    def front(kind, c, g, par, h, job):
                        bank, n, _ = job
                        if kind == "xt":
                            dve.wait_ge(xt_hi, g + 1)
                            nc.vector.tensor_tensor(xT[1][:], R[:, bank, :], xT[0][:].bitcast(F32),
                                                    ALU.subtract).then_inc(ring_done[bank], 1)
                        elif kind == "ct":
                            dve.wait_ge(ct_hi, g + 1)
                            nc.vector.tensor_tensor(cT[1][:], R[:, bank, 0:KW], cT[0][:].bitcast(F32),
                                                    ALU.subtract).then_inc(ring_done[bank], 1)
                        elif kind == "q" and small:
                            dve.wait_ge(qk_hi, 2 * QC * g + QC + c + 1)
                            nc.vector.scalar_tensor_tensor(qT[:, par, c, :], R[:, bank, :], sgn[:, 0:1],
                                                           rounded[:, bank, :].bitcast(F32), ALU.mult,
                                                           ALU.subtract).then_inc(ring_done[bank], 1)
                        elif kind == "q":
                            dve.wait_ge(ring_full[bank], n + 1)
                            nc.vector.tensor_copy(qT[:, par, c, :], R[:, bank, :]).then_inc(ring_done[bank], 1)
                        elif kind == "k" and small:
                            dve.wait_ge(qk_hi, 2 * QC * g + c + 1)
                            need(dve, kbd_done, 4 * (QC * (g - 1) + c + 1))
                            nc.vector.scalar_tensor_tensor(kst[:, c, :], R[:, bank, 0:KW], sgn[:, 1:2],
                                                           rounded[:, bank, 0:KW].bitcast(F32), ALU.mult,
                                                           ALU.subtract).then_inc(ring_done[bank], 1)

                    @staticmethod
                    def norm(g, par, h):
                        if x_in is not None:
                            dve.wait_ge(x_loaded[par], 16 * h + 16)
                        norm.statistics(dve, g)

                    @staticmethod
                    def scaling(g):
                        norm.scaling(dve, g)

                    @staticmethod
                    def scores(u, st, par, g):
                        dve.wait_ge(s_full, u + 1)
                        s = S[:, :, 0:4 * KL].rearrange("p b (h k) -> p b h k", h=4)
                        nc.vector.tensor_reduce(nmax[:, st % 2, :].rearrange("p (b h) -> p b h", b=2), s,
                                                AX.X, ALU.max).then_inc(max_done, 1)
                        dve.wait_ge(max_done, u + 1)
                        nc.vector.tensor_tensor(
                            Sm[:, st % 2].rearrange("p (b h) k -> p b h k", b=2), s,
                            nmax[:, st % 2, :].rearrange("p (b h) -> p b h", b=2).unsqueeze(3).to_broadcast([P, 2, 4, KL]),
                            ALU.subtract).then_inc(sub_done, 1)

                    transposes = staticmethod(lambda *a: None)

                    @staticmethod
                    def values(u, st, par, cc, job):
                        bank, n, _ = job
                        dve.wait_ge(ring_full[bank], n + 1)
                        r = (st + cc) % 2 if small else cc
                        at = (UH - 1) * VW if small and place(st)[1] else 0
                        o = R[:, bank, at:at + OH * VW].rearrange("p (h w) -> p h w", w=VW)
                        nc.vector.reciprocal(rden[:, r, :], o[:, :, DH]).then_inc(rec_done, 1)
                        dve.wait_ge(rec_done, (UH // OH) * u + cc + 1)
                        j, half = place(st)
                        out = O[:, par, j, half * UH:(half + 1) * UH, :] if small else \
                            O[:, st % 2, cc * OH:(cc + 1) * OH, :]
                        nc.vector.tensor_tensor(out, o[:, :, 0:DH],
                                                rden[:, r, :].unsqueeze(2).to_broadcast([P, OH, DH]),
                                                ALU.mult).then_inc(ring_done[bank], 1)

                    @staticmethod
                    def tail(kind, c, g, par, job):
                        bank, n, _ = job
                        if kind == "ot":
                            dve.wait_ge(ot_hi, OTJ * g + c + 1)
                            nc.vector.tensor_tensor(ot_slot(OT[1], c), ot_job(bank),
                                                    ot_slot(OT[0], c).bitcast(F32),
                                                    ALU.subtract).then_inc(ring_done[bank], 1)
                        elif kind == "y" and c % 2:
                            dve.wait_ge(ring_full[bank], n + 1)
                            nc.vector.tensor_tensor(yT[:], R[:, bank, 0:SQ * P], yT[:], ALU.add
                                                    ).then_inc(ring_done[bank], 1)
                        elif kind == "yt":
                            dve.wait_ge(ring_full[bank], n + 1)
                            sq = g * GB + c * SQ
                            x = X[:, bass.ds(sq, SQ), :]
                            nc.vector.tensor_tensor(x, R[:, bank, 0:SQ * P].rearrange("p (s d) -> p s d", s=SQ),
                                                    x, ALU.add).then_inc(ring_done[bank], 1)
                            wait_apart(dve, const, ring_done[bank], n + 1)
                            for j in range(SQ):
                                nc.vector.bn_stats(st_new[:, j, :], X[:, sq + j, :]).then_inc(
                                    x_done if j == SQ - 1 else new_stats, 1)
                            wait_apart(dve, const, x_done, YT * g + c + 1)
                            for j in range(SQ):
                                nc.vector.bn_aggr(mv_new[:, j, :], st_new[:, j, :]).then_inc(new_stats, 1)
                            dve.wait_ge(new_stats, (2 * SQ - 1) * (YT * g + c + 1))
                            nc.vector.tensor_copy(MV[:, bass.ds(sq, SQ), :], mv_new[:, 0:SQ, :]).then_inc(mv_done, 1)

                walk(dve, do)

            @block.tensor
            def _(pe):
                seen = {}

                def wait_jobs(bank, *keys):
                    places = sorted(seen[key] for key in keys)
                    for b in range(RB):
                        at = [p for p in places if p % RB == b]
                        if at and b != bank:
                            pe.wait_ge(ring_done[b], ring_base[0] + at[-1] // RB + 1)

                class do:
                    @staticmethod
                    def front(kind, c, g, par, h, job):
                        bank, n, _ = job
                        seen[kind, c] = job[2]
                        need(pe, ring_done[bank], n)
                        if kind == "xt":
                            pe.wait_ge(norm.xn_done, GB * (g + 1))
                            for j in range(GB):
                                last = pe.transpose(R[:, bank, j * P:(j + 1) * P], norm.xn[:, j, :],
                                                    const.ident[:])
                        elif kind == "ct":
                            pe.wait_ge(ctx_loaded, 16 * g + 16)
                            for j in range(GB):
                                last = pe.transpose(R[:, bank, j * KL:(j + 1) * KL], cx[:, j, :],
                                                    const.ident[0:KL, 0:KL])
                        elif kind == "q":
                            if c == 0:
                                wait_jobs(bank, ("xt", 0))
                            w = [W[:, c * P:(c + 1) * P] for W in WQ]
                            last = passes(nc, R[:, bank, :], w, [x[:] for x in xT])
                        elif kind == "k":
                            if c == 0:
                                wait_jobs(bank, ("ct", 0))
                            w = [W[:, c * P:(c + 1) * P] for W in WK]
                            last = passes(nc, R[:, bank, 0:KW], w, [x[:] for x in cT])
                        elif small:
                            for j in range(GB):
                                ct = [x[:, j * KL:(j + 1) * KL] for x in cT]
                                last = passes(nc, R[0:KL, bank, j * P:(j + 1) * P], ct, [W[:] for W in WV])
                        else:
                            ct = [x[:, (c // 2) * KL:(c // 2 + 1) * KL] for x in cT]
                            last = passes(nc, R[0:KL, bank, :], ct,
                                          [W[:, (c % 2) * 512:(c % 2 + 1) * 512] for W in WV])
                        last.then_inc(ring_full[bank], 1)

                    @staticmethod
                    def scores(u, st, par, g):
                        if st == 0:
                            wait_jobs(None, *[(kind, c) for kind in "qk" for c in range(max(0, QC - RB), QC)])
                            if small:
                                pe.wait_ge(kbd_done, 4 * QC * (g + 1))
                            else:
                                pe.wait_ge(mask_done, g + 1)
                        need(pe, sub_done, u)
                        j, half = place(st)
                        for b in range(2):
                            if not small:
                                pe.matmul(S[:, b, 0:4 * KL], const.ident_bf[:],
                                          mb[:, par, j, :].unsqueeze(1).to_broadcast([P, 4, KL]),
                                          start=True, stop=False, skip_group_check=True)
                            for i in range(CPB):
                                c = (2 * half + b) * CPB + i
                                last = pe.matmul(S[:, b, i * KBW:(i + 1) * KBW],
                                                 qT[:, par, c, j * P:(j + 1) * P], kbd[:, par, c, j, :],
                                                 start=small, stop=True, skip_group_check=not small)
                        last.then_inc(s_full, 1)

                    @staticmethod
                    def transposes(u, st):
                        pe.wait_ge(exp_done, u + 1)
                        for cc in range(2):
                            for k in range(4):
                                last = pe.transpose(PT[0:KL, cc, k * P:(k + 1) * P], Sm[:, st % 2, 4 * cc + k, :],
                                                    const.ident[:])
                            last.then_inc(pt_full, 1)

                    @staticmethod
                    def values(u, st, par, cc, job):
                        bank, n, _ = job
                        seen["o", st, cc] = job[2]
                        need(pe, ring_done[bank], n)
                        pe.wait_ge(pt_done, 2 * u + (cc + 1) * OH // 4)
                        if st == 0 and cc == 0:
                            wait_jobs(bank, *[("v", c) for c in range(max(0, NV - RB), NV)])
                        j, half = place(st)
                        wide = UH if small else 1
                        for k in (range(OH - 1, -1, -1) if small and half else range(OH)):
                            slot = cc * OH + k
                            head = UH * half + slot - (wide - 1) * half
                            last = pe.matmul(R[:, bank, k * VW:(k + wide) * VW],
                                             PTs[:, st % 2, slot // 4, slot % 4 * P:(slot % 4 + 1) * P],
                                             V[:, par, j, head:head + wide, :].rearrange("p h w -> p (h w)"),
                                             start=True, stop=True)
                        last.then_inc(ring_full[bank], 1)

                    @staticmethod
                    def tail(kind, c, g, par, job):
                        bank, n, _ = job
                        seen[kind, c] = job[2]
                        need(pe, ring_done[bank], n)
                        if kind == "ot":
                            wait_jobs(bank, *([("o", UPG - 1, 0)] if small else [("o", c, 0), ("o", c, 1)]))
                            for k in range(4):
                                o = O[:, par, k] if small else O[:, c % 2, 2 * k:2 * k + 2]
                                last = pe.transpose(R[:, bank, k * P:(k + 1) * P],
                                                    o.rearrange("p h w -> p (h w)"), const.ident[:])
                        elif kind == "y":
                            jobs = [("ot", 0)] if small else [("ot", 2 * c), ("ot", 2 * c + 1)]
                            wait_jobs(bank, *(jobs + ([("y", c - 1)] if c % 2 else [])))
                            chunks = [0] if small else range(c % 2 * 4, c % 2 * 4 + 4)
                            for k, ch in enumerate(chunks):
                                last = passes(nc, R[:, bank, 0:SQ * P], [W[:, ch * P:(ch + 1) * P] for W in WO],
                                              [x[:, k, :] for x in OT], start=k == 0, stop=k == len(chunks) - 1)
                        else:
                            wait_jobs(bank, ("y", 0 if small else 2 * c + 1))
                            for k in range(SQ):
                                last = pe.transpose(R[:, bank, k * P:(k + 1) * P], yT[:, k * P:(k + 1) * P],
                                                    const.ident[:])
                        last.then_inc(ring_full[bank], 1)

                    norm = scaling = staticmethod(lambda *a: None)

                pe.wait_ge(ready, 3)
                walk(pe, do)


def normalise_all(nc, const, X, MV, layer, XT, LG, gate_w, gate_b):
    tag = f"N{layer}_"
    with ExitStack() as ctx:
        def sb(name, shape, dt):
            return ctx.enter_context(nc.sbuf_tensor(tag + name, shape, dt))

        def sem(name):
            return ctx.enter_context(nc.semaphore(tag + name))

        T = ctx.enter_context(nc.psum_tensor(tag + "T", [P, 2, 512], F32))
        L = ctx.enter_context(nc.psum_tensor(tag + "L", [P, 2, 512], F32))
        U = ctx.enter_context(nc.psum_tensor(tag + "U", [P, 2, 512], F32))
        ve = sb("ve", [P, NB], F32)
        rstd = sb("rstd", [P, NB], F32)
        xn = sb("xn", [P, 2, GB, P], F32)
        gw_raw = sb("gw_raw", [P, P], F32)
        GW = [sb(f"GW{i}", [P, P], F32R) for i in range(2)]
        gb = sb("gb", [NE, 1], F32)
        lgT = sb("lgT", [NE, 2, 512], F32)
        ve_done = sem("ve_done")
        rstd_done = sem("rstd_done")
        cleared = sem("cleared")
        gate_loaded = sem("gate_loaded")
        prepared = sem("prepared")
        xn_done = sem("xn_done")
        t_full = sem("t_full")
        hi_done = sem("hi_done")
        lo_done = sem("lo_done")
        l_full = sem("l_full")
        l_done = sem("l_done")
        u_full = sem("u_full")
        u_done = sem("u_done")

        def walk(eng, do):
            do.tiles(0, 0)
            for g in range(3):
                do.tiles(g + 1, (g + 1) % 2)
                do.logits(g, g % 2)
            with eng.Fori(2, NG // 2) as h:
                do.tiles(2 * h, 0)
                do.logits(2 * h - 1, 1)
                do.tiles(2 * h + 1, 1)
                do.logits(2 * h, 0)
            do.rest()

        with nc.Block() as block:
            @block.sync
            def _(sp):
                sp.wait_ge(cleared, 1)
                sp.dma_start(gw_raw[:, 0:NE], gate_w).then_inc(gate_loaded, 16)
                sp.dma_start(gb[:], gate_b.unsqueeze(1)).then_inc(gate_loaded, 16)

            @block.gpsimd
            def _(pool):
                pool.wait_ge(ve_done, 1)
                for g in range(NG):
                    cols = slice(g * GB, (g + 1) * GB)
                    nc.gpsimd.tensor_tensor(rstd[:, cols], ve[:, cols], const.minus_half[:, cols],
                                            ALU.pow).then_inc(rstd_done, 1)

            @block.vector
            def _(dve):
                def low(g, par):
                    dve.wait_ge(hi_done, g + 1)
                    nc.vector.tensor_tensor(XT[1][:, bass.ds(g * 512, 512)], T[:, par, :],
                                            XT[0][:, bass.ds(g * 512, 512)].bitcast(F32),
                                            ALU.subtract).then_inc(lo_done, 1)

                def keep(g, par):
                    dve.wait_ge(u_full, g + 1)
                    nc.vector.tensor_copy(LG[:, bass.ds(g * GB, GB), :],
                                          U[:, par, 0:GB * NE].rearrange("p (b e) -> p b e", e=NE)
                                          ).then_inc(u_done, 1)

                class do:
                    @staticmethod
                    def tiles(g, par):
                        dve.wait_ge(rstd_done, g + 1)
                        need(dve, t_full, g - 1)
                        for j in range(GB):
                            t = g * GB + j
                            nc.vector.tensor_scalar(xn[:, par, j, :], X[:, t, :], MV[:, t, 0:1],
                                                    rstd[:, bass.ds(t, 1)], ALU.subtract,
                                                    ALU.mult).then_inc(xn_done, 1)
                        if not isinstance(g, int) or g:
                            low(g - 1, 1 - par)

                    @staticmethod
                    def logits(g, par):
                        if not isinstance(g, int) or g >= 2:
                            keep(g - 2, par)

                    @staticmethod
                    def rest():
                        low(NG - 1, 1)
                        keep(NG - 3, 1)
                        keep(NG - 2, 0)
                        keep(NG - 1, 1)

                nc.vector.memset(gw_raw[:], 0.0).then_inc(cleared, 1)
                nc.vector.tensor_scalar(ve[:], MV[:, :, 1], EPS, None, ALU.add).then_inc(ve_done, 1)
                dve.wait_ge(gate_loaded, 32)
                split(nc, GW[0][:], GW[1][:], gw_raw[:], prepared, 0)
                walk(dve, do)
                dve.wait_ge(u_done, NG)

            @block.scalar
            def _(act):
                class do:
                    @staticmethod
                    def tiles(g, par):
                        wait_apart(act, const, t_full, g + 1)
                        nc.scalar.copy(XT[0][:, bass.ds(g * 512, 512)], T[:, par, :]).then_inc(hi_done, 1)

                    @staticmethod
                    def logits(g, par):
                        act.wait_ge(l_full, g + 1)
                        nc.scalar.activation(lgT[:, par, :], L[0:NE, par, :], ACT.Identity, bias=gb[:]
                                             ).then_inc(l_done, 1)

                    @staticmethod
                    def rest():
                        do.logits(NG - 1, 1)

                act.wait_ge(gate_loaded, 32)
                walk(act, do)

            @block.tensor
            def _(pe):
                class do:
                    @staticmethod
                    def tiles(g, par):
                        pe.wait_ge(xn_done, GB * (g + 1))
                        need(pe, lo_done, g - 1)
                        for j in range(GB):
                            last = pe.transpose(T[:, par, j * P:(j + 1) * P], xn[:, par, j, :], const.ident[:])
                        last.then_inc(t_full, 1)

                    @staticmethod
                    def logits(g, par):
                        pe.wait_ge(lo_done, g + 1)
                        passes(nc, L[:, par, :], [W[:] for W in GW],
                               [x[:, bass.ds(g * 512, 512)] for x in XT]).then_inc(l_full, 1)
                        if not isinstance(g, int) or g:
                            turn(g - 1, 1 - par)

                    @staticmethod
                    def rest():
                        do.logits(NG - 1, 1)
                        turn(NG - 1, 1)

                def turn(g, par):
                    need(pe, u_done, g - 1)
                    wait_apart(pe, const, l_done, g + 1)
                    for j in range(GB):
                        last = pe.transpose(U[:, par, j * NE:(j + 1) * NE], lgT[:, par, j * P:(j + 1) * P],
                                            const.ident[0:NE, 0:NE])
                    last.then_inc(u_full, 1)

                pe.wait_ge(prepared, 2)
                walk(pe, do)


def gate_scale(nc, LG, scale, gate_scale_in):
    N = NB * NE
    tag = "G_"
    with ExitStack() as ctx:
        def sb(name, shape):
            return ctx.enter_context(nc.sbuf_tensor(tag + name, shape, F32))

        rw = sb("rw", [P, NE])
        t = sb("t", [P, NB, NE])
        m = sb("m", [P, NB])
        r = sb("r", [P, NB])
        half = sb("half", [P, NB])
        loaded = ctx.enter_context(nc.semaphore(tag + "loaded"))
        v = ctx.enter_context(nc.semaphore(tag + "v"))
        a = ctx.enter_context(nc.semaphore(tag + "a"))
        q = ctx.enter_context(nc.semaphore(tag + "q"))
        wide = [P, NB, NE]

        with nc.Block() as block:
            @block.sync
            def _(sp):
                sp.dma_start(rw[:], gate_scale_in.partition_broadcast(P)).then_inc(loaded, 16)

            @block.gpsimd
            def _(pool):
                pool.wait_ge(v, 4)
                nc.gpsimd.tensor_tensor(r[:], m[:], half[:], ALU.pow).then_inc(q, 1)

            @block.scalar
            def _(act):
                act.wait_ge(v, 8)
                tt = t[:].rearrange("p b e -> p (b e)")
                nc.scalar.activation(tt, tt, ACT.Exp, scale=2.0).then_inc(a, 1)

            @block.vector
            def _(dve):
                dve.wait_ge(loaded, 16)
                nc.vector.memset(half[:], -0.5).then_inc(v, 1)
                nc.vector.tensor_tensor(t[:], LG[:], LG[:], ALU.mult).then_inc(v, 1)
                dve.wait_ge(v, 2)
                nc.vector.tensor_reduce(m[:], t[:], AX.X, ALU.add).then_inc(v, 1)
                dve.wait_ge(v, 3)
                nc.vector.tensor_scalar(m[:], m[:], 1.0 / NE, 1.1920928955078125e-07, ALU.mult, ALU.add
                                        ).then_inc(v, 1)
                dve.wait_ge(q, 1)
                nc.vector.tensor_tensor(t[:], LG[:], r[:].unsqueeze(2).to_broadcast(wide), ALU.mult).then_inc(v, 1)
                dve.wait_ge(v, 5)
                nc.vector.tensor_tensor(t[:], t[:], rw[:].unsqueeze(1).to_broadcast(wide), ALU.mult).then_inc(v, 1)
                dve.wait_ge(v, 6)
                nc.vector.tensor_reduce(m[:], t[:], AX.X, ALU.max).then_inc(v, 1)
                dve.wait_ge(v, 7)
                nc.vector.tensor_tensor(t[:], t[:], m[:].unsqueeze(2).to_broadcast(wide), ALU.subtract).then_inc(v, 1)
                dve.wait_ge(a, 1)
                nc.vector.tensor_reduce(m[:], t[:], AX.X, ALU.add).then_inc(v, 1)
                dve.wait_ge(v, 9)
                nc.vector.reciprocal(m[:], m[:]).then_inc(v, 1)
                dve.wait_ge(v, 10)
                nc.vector.tensor_scalar(r[:], m[:], 1e-6, None, ALU.add).then_inc(v, 1)
                dve.wait_ge(v, 11)
                nc.vector.reciprocal(r[:], r[:]).then_inc(v, 1)
                dve.wait_ge(v, 12)
                nc.vector.tensor_tensor(scale[:], m[:], r[:], ALU.mult).then_inc(v, 1)
                dve.wait_ge(v, 13)


def top2_weights(nc, LG, WT, rank_in):
    tag = "T_"
    with ExitStack() as ctx:
        def sb(name, shape):
            return ctx.enter_context(nc.sbuf_tensor(tag + name, shape, F32))

        rank = sb("rank", [P, NE])
        l2 = sb("l2", [P, NB, NE])
        e = [sb(f"e{i}", [P, NB, NE]) for i in range(2)]
        m = [sb(f"m{i}", [P, NB]) for i in range(2)]
        k = sb("k", [P, NB])
        d = sb("d", [P, NB])
        loaded = ctx.enter_context(nc.semaphore(tag + "loaded"))
        v = ctx.enter_context(nc.semaphore(tag + "v"))
        a = ctx.enter_context(nc.semaphore(tag + "a"))
        wide = [P, NB, NE]

        with nc.Block() as block:
            @block.sync
            def _(sp):
                sp.dma_start(rank[:], rank_in.partition_broadcast(P)).then_inc(loaded, 16)

            @block.scalar
            def _(act):
                act.wait_ge(v, 12)
                nc.scalar.activation(d[:], d[:], ACT.Exp).then_inc(a, 1)

            @block.vector
            def _(dve):
                dve.wait_ge(loaded, 16)

                def b(x):
                    return x[:].unsqueeze(2).to_broadcast(wide)

                n = 0
                for i, src in ((0, LG), (1, l2)):
                    nc.vector.tensor_reduce(m[i][:], src[:], AX.X, ALU.max).then_inc(v, 1)
                    dve.wait_ge(v, n + 1)
                    nc.vector.tensor_tensor(e[i][:], src[:], b(m[i]), ALU.is_equal).then_inc(v, 1)
                    dve.wait_ge(v, n + 2)
                    nc.vector.tensor_tensor(e[i][:], e[i][:], rank[:].unsqueeze(1).to_broadcast(wide),
                                            ALU.mult).then_inc(v, 1)
                    dve.wait_ge(v, n + 3)
                    nc.vector.tensor_reduce(k[:], e[i][:], AX.X, ALU.max).then_inc(v, 1)
                    dve.wait_ge(v, n + 4)
                    nc.vector.tensor_tensor(e[i][:], e[i][:], b(k), ALU.is_equal).then_inc(v, 1)
                    dve.wait_ge(v, n + 5)
                    n += 5
                    if i == 0:
                        nc.vector.scalar_tensor_tensor(l2[:], e[0][:], MASKED, LG[:], ALU.mult,
                                                       ALU.add).then_inc(v, 1)
                        dve.wait_ge(v, n + 1)
                        n += 1
                nc.vector.tensor_tensor(d[:], m[1][:], m[0][:], ALU.subtract).then_inc(v, 1)
                dve.wait_ge(a, 1)
                nc.vector.tensor_scalar(k[:], d[:], 1.0, None, ALU.add).then_inc(v, 1)
                dve.wait_ge(v, n + 2)
                nc.vector.reciprocal(m[0][:], k[:]).then_inc(v, 1)
                dve.wait_ge(v, n + 3)
                nc.vector.tensor_tensor(m[1][:], d[:], m[0][:], ALU.mult).then_inc(v, 1)
                dve.wait_ge(v, n + 4)
                for i in range(2):
                    nc.vector.tensor_tensor(e[i][:], e[i][:], b(m[i]), ALU.mult).then_inc(v, 1)
                dve.wait_ge(v, n + 6)
                nc.vector.tensor_tensor(WT[:], e[0][:], e[1][:], ALU.add).then_inc(v, 1)
                dve.wait_ge(v, n + 7)


def dense_experts(nc, const, X, XT, scale, w1, b1, w2, b2):
    H = 256
    NC = NE * H // P
    BT = 512
    tag = "E0_"
    with ExitStack() as ctx:
        def sb(name, shape, dt):
            return ctx.enter_context(nc.sbuf_tensor(tag + name, shape, dt))

        def sem(name):
            return ctx.enter_context(nc.semaphore(tag + name))

        U = ctx.enter_context(nc.psum_tensor(tag + "U", [P, 4, 512], F32))
        Y = ctx.enter_context(nc.psum_tensor(tag + "Y", [P, 2, 512], F32))
        T = ctx.enter_context(nc.psum_tensor(tag + "T", [P, 2, 512], F32))
        raw = sb("raw", [P, 2, NC * P], F32)
        W1 = [sb(f"W1{i}", [P, NC * P], F32R) for i in range(2)]
        W2 = [sb(f"W2{i}", [P, NC * P], F32R) for i in range(2)]
        B1 = sb("B1", [P, NC], F32)
        B2 = sb("B2", [P, NE], F32)
        b2sum = sb("b2sum", [P, 1], F32)
        G = sb("G", [P, 4, BT], F32)
        GP = [sb(f"GP{i}", [P, 4, BT], F32R) for i in range(2)]
        yT = sb("yT", [P, 2, BT], F32)
        w_loaded = sem("w_loaded")
        prepared = sem("prepared")
        u_full = sem("u_full")
        g_done = sem("g_done")
        h_done = sem("h_done")
        l_done = sem("l_done")
        d_done = sem("d_done")
        y_done = sem("y_done")
        t_full = sem("t_full")
        x_done = sem("x_done")

        def walk(eng, do):
            def pair(h, last):
                for par in range(2):
                    blk = 2 * h + par
                    for c in range(NC):
                        n = blk * NC + c
                        ahead = c + 2 >= NC
                        if not (last and par == 1 and ahead):
                            do.up(n + 2, (c + 2) % NC, blk + 1 if ahead else blk)
                        do.down(n, c, par, blk)
                        if c == 3 and not (isinstance(blk, int) and blk == 0):
                            do.finish(blk - 1, 1 - par)

            do.up(0, 0, 0)
            do.up(1, 1, 0)
            pair(0, False)
            with eng.Fori(1, NG // 2 - 1) as h:
                pair(h, False)
            pair(NG // 2 - 1, True)
            do.finish(NG - 1, 1)

        with nc.Block() as block:
            @block.sync
            def _(sp):
                sp.dma_start(raw[:, 0, :].rearrange("p (e h) -> p e h", e=NE),
                             w1.rearrange("e d h -> d e h")).then_inc(w_loaded, 16)
                sp.dma_start(raw[:, 1, :].rearrange("p (c d) -> p c d", c=NC),
                             w2.rearrange("e (c p) d -> p (e c) d", p=P)).then_inc(w_loaded, 16)
                sp.dma_start(B1[:], b1).then_inc(w_loaded, 16)
                sp.dma_start(B2[:], b2).then_inc(w_loaded, 16)

            @block.vector
            def _(dve):
                dve.wait_ge(w_loaded, 64)
                at = split(nc, W1[0][:], W1[1][:], raw[:, 0, :], prepared, 0)
                at = split(nc, W2[0][:], W2[1][:], raw[:, 1, :], prepared, at)
                nc.vector.tensor_reduce(b2sum[:], B2[:], AX.X, ALU.add).then_inc(prepared, 1)

                class do:
                    up = staticmethod(lambda *a: None)

                    @staticmethod
                    def down(n, c, par, blk):
                        dve.wait_ge(g_done, n + 1)
                        need(dve, d_done, n - 3)
                        nc.vector.tensor_copy(GP[0][:, c % 4, :], G[:, c % 4, :]).then_inc(h_done, 1)
                        dve.wait_ge(h_done, n + 1)
                        nc.vector.tensor_tensor(GP[1][:, c % 4, :], G[:, c % 4, :],
                                                GP[0][:, c % 4, :].bitcast(F32), ALU.subtract).then_inc(l_done, 1)

                    @staticmethod
                    def finish(blk, par):
                        dve.wait_ge(t_full, blk + 1)
                        for j in range(GB):
                            t = blk * GB + j
                            nc.vector.scalar_tensor_tensor(X[:, t, :], T[:, par, j * P:(j + 1) * P],
                                                           scale[:, bass.ds(t, 1)], X[:, t, :], ALU.mult,
                                                           ALU.add).then_inc(x_done, 1)

                walk(dve, do)
                dve.wait_ge(x_done, NB)

            @block.scalar
            def _(act):
                class do:
                    up = staticmethod(lambda *a: None)

                    @staticmethod
                    def down(n, c, par, blk):
                        act.wait_ge(u_full, n + 1)
                        need(act, l_done, n - 3)
                        nc.scalar.activation(G[:, c % 4, :], U[:, c % 4, :], ACT.Gelu, bias=B1[:, c:c + 1]
                                             ).then_inc(g_done, 1)
                        if c == 2:
                            self_finish(blk - 1, 1 - par)

                    finish = staticmethod(lambda *a: None)

                def self_finish(blk, par):
                    if isinstance(blk, int) and blk < 0:
                        return
                    act.wait_ge(d_done, (blk + 1) * NC)
                    nc.scalar.activation(yT[:, par, :], Y[:, par, :], ACT.Identity, bias=b2sum[:]
                                         ).then_inc(y_done, 1)

                act.wait_ge(prepared, 5)
                walk(act, do)
                self_finish(NG - 1, 1)

            @block.tensor
            def _(pe):
                class do:
                    @staticmethod
                    def up(n, c, blk):
                        need(pe, g_done, n - 3)
                        passes(nc, U[:, c % 4, :], [W[:, c * P:(c + 1) * P] for W in W1],
                               [x[:, bass.ds(blk * BT, BT)] for x in XT]).then_inc(u_full, 1)

                    @staticmethod
                    def down(n, c, par, blk):
                        pe.wait_ge(l_done, n + 1)
                        if c == 0:
                            need(pe, y_done, blk - 1)
                        passes(nc, Y[:, par, :], [W[:, c * P:(c + 1) * P] for W in W2],
                               [g[:, c % 4, :] for g in GP], start=c == 0, stop=c == NC - 1).then_inc(d_done, 1)

                    @staticmethod
                    def finish(blk, par):
                        pe.wait_ge(y_done, blk + 1)
                        need(pe, x_done, GB * (blk - 1))
                        for j in range(GB):
                            last = pe.transpose(T[:, par, j * P:(j + 1) * P], yT[:, par, j * P:(j + 1) * P],
                                                const.ident[:])
                        last.then_inc(t_full, 1)

                pe.wait_ge(prepared, 5)
                walk(pe, do)


def routed_experts(nc, const, X, XT, WT, w1, b1, w2, b2, out):
    H = 512
    NC = H // P
    BT = 512
    tag = "E1_"
    with ExitStack() as ctx:
        def sb(name, shape, dt):
            return ctx.enter_context(nc.sbuf_tensor(tag + name, shape, dt))

        def sem(name):
            return ctx.enter_context(nc.semaphore(tag + name))

        U = ctx.enter_context(nc.psum_tensor(tag + "U", [P, 3, 2, 512], F32))
        Y = ctx.enter_context(nc.psum_tensor(tag + "Y", [P, 2, 512], F32))
        raw1 = sb("raw1", [P, 2 * H], F32)
        raw2 = sb("raw2", [P, NC, P], F32)
        W1 = [sb(f"W1{i}", [P, 2, 2 * H], F32R) for i in range(2)]
        W2 = [sb(f"W2{i}", [P, 2, H], F32R) for i in range(2)]
        B1 = sb("B1", [P, NE * 2 * NC], F32)
        B2 = sb("B2", [P, NE], F32)
        SL = sb("SL", [P, 3, BT], F32)
        G = sb("G", [P, 3, BT], F32)
        GP = [sb(f"GP{i}", [P, 3, BT], F32R) for i in range(2)]
        yT = sb("yT", [P, BT], F32)
        b_loaded = sem("b_loaded")
        w_loaded = [sem(f"w_loaded{i}") for i in range(2)]
        w_split = sem("w_split")
        u_full = sem("u_full")
        s_done = sem("s_done")
        g_done = sem("g_done")
        h_done = sem("h_done")
        l_done = sem("l_done")
        d_done = sem("d_done")
        y_done = sem("y_done")
        t_full = sem("t_full")
        x_done = sem("x_done")
        stored = sem("stored")

        def walk(eng, do):

            def ahead(stage, n, k, e, ep, blk0, final):
                blk, c = blk0 + k // NC, k % NC
                if isinstance(blk, int) and blk >= NG:
                    if final:
                        return
                    if blk == NG and c == 0 and stage == do.up:
                        do.next_weights(e + 1, 1 - ep)
                    stage(n, slot(k), c, blk - NG, e + 1, 1 - ep)
                else:
                    stage(n, slot(k), c, blk, e, ep)

            first_slot = [0]

            def slot(k):
                return (first_slot[0] + k) % 3

            def blocks(e, ep, blk0, odd, count, first, final):
                for k in range(count * NC):
                    m, c, par = e * NG + blk0 + k // NC, k % NC, (odd + k // NC) % 2
                    n = (e * NG + blk0) * NC + k
                    ahead(do.up, n + 3, k + 3, e, ep, blk0, final)
                    ahead(do.gate, n + 1, k + 1, e, ep, blk0, final)
                    do.down(n, slot(k), c, m, par, e, ep)
                    if c == do.finish_at and not first:
                        if isinstance(blk0, int) and blk0 + k // NC == 0:
                            do.finish(m - 1, 1 - par, NG - 1, e - 1)
                        else:
                            do.finish(m - 1, 1 - par, blk0 + k // NC - 1, e)
                first_slot[0] = (first_slot[0] + count * NC) % 3

            def expert(e, ep, first, final):
                blocks(e, ep, 0, 0, 1, first, False)
                with eng.Fori(0, (NG - 1) // 6) as h:
                    blocks(e, ep, 6 * h + 1, 1, 6, False, False)
                done = 1 + (NG - 1) // 6 * 6
                blocks(e, ep, done, done % 2, NG - done, False, final)

            do.next_weights(0, 0)
            for k in range(3):
                do.up(k, k, k, 0, 0, 0)
            do.gate(0, 0, 0, 0, 0, 0)
            for e in range(NE):
                expert(e, e % 2, e == 0, e == NE - 1)
            do.finish(NE * NG - 1, 1, NG - 1, NE - 1)

        def nothing(*a):
            return None

        with nc.Block() as block:
            @block.sync
            def _(sp):
                sp.dma_start(B1[:], b1).then_inc(b_loaded, 16)
                sp.dma_start(B2[:], b2).then_inc(b_loaded, 16)
                for e in range(NE):
                    if e:
                        sp.wait_ge(w_split, 4 * e)
                    sp.dma_start(raw1[:], w1[e]).then_inc(w_loaded[e % 2], 16)
                    sp.dma_start(raw2[:], w2[e].rearrange("(c p) d -> p c d", p=P)).then_inc(w_loaded[e % 2], 16)
                with sp.Fori(0, NG) as g:
                    sp.wait_ge(x_done, (NE - 1) * NB + GB * (g + 1))
                    sp.dma_start(out[bass.ds(g * GB, GB)].rearrange("b s d -> s b d"),
                                 X[:, bass.ds(g * GB, GB), :]).then_inc(stored, 16)
                sp.wait_ge(stored, 16 * NG)

            @block.vector
            def _(dve):
                class do:
                    finish_at = 3
                    @staticmethod
                    def next_weights(e, ep):
                        dve.wait_ge(w_loaded[ep], 32 * (e // 2) + 32)
                        for i, (W, r) in enumerate(((W1, raw1[:]), (W2, raw2[:].rearrange("p c d -> p (c d)")))):
                            nc.vector.tensor_copy(W[0][:, ep, :], r).then_inc(w_split, 1)
                            dve.wait_ge(w_split, 4 * e + 2 * i + 1)
                            nc.vector.tensor_tensor(W[1][:, ep, :], r, W[0][:, ep, :].bitcast(F32),
                                                    ALU.subtract).then_inc(w_split, 1)

                    up = staticmethod(nothing)

                    @staticmethod
                    def gate(n, q, c, blk, e, ep):
                        need(dve, l_done, n - 2)
                        dve.wait_ge(s_done, n + 1)
                        bias = B1[:, bass.ds(e * 2 * NC + NC + c, 1)]
                        nc.vector.scalar_tensor_tensor(G[:, q, :], U[:, q, 1, :], bias, SL[:, q, :],
                                                       ALU.add, ALU.mult).then_inc(g_done, 1)

                    @staticmethod
                    def down(n, q, c, m, par, e, ep):
                        dve.wait_ge(h_done, n + 1)
                        nc.vector.tensor_tensor(GP[1][:, q, :], G[:, q, :],
                                                GP[0][:, q, :].bitcast(F32), ALU.subtract).then_inc(l_done, 1)

                    @staticmethod
                    def finish(m, par, blk, e):
                        dve.wait_ge(t_full, m + 1)
                        need(dve, x_done, GB * m)
                        for j in range(GB):
                            t = blk * GB + j
                            nc.vector.scalar_tensor_tensor(X[:, t, :], Y[:, par, j * P:(j + 1) * P],
                                                           WT[:, t, bass.ds(e, 1)], X[:, t, :], ALU.mult,
                                                           ALU.add).then_inc(x_done, 1)

                dve.wait_ge(b_loaded, 32)
                walk(dve, do)

            @block.scalar
            def _(act):
                class do:
                    finish_at = 1
                    up = next_weights = staticmethod(nothing)

                    @staticmethod
                    def gate(n, q, c, blk, e, ep):
                        act.wait_ge(u_full, n + 1)
                        wait_apart(act, const, g_done, n - 2)
                        nc.scalar.activation(SL[:, q, :], U[:, q, 0, :], ACT.Silu,
                                             bias=B1[:, bass.ds(e * 2 * NC + c, 1)]).then_inc(s_done, 1)

                    @staticmethod
                    def down(n, q, c, m, par, e, ep):
                        act.wait_ge(g_done, n + 1)
                        need(act, d_done, n - 2)
                        nc.scalar.copy(GP[0][:, q, :], G[:, q, :]).then_inc(h_done, 1)

                    @staticmethod
                    def finish(m, par, blk, e):
                        wait_apart(act, const, d_done, (m + 1) * NC)
                        wait_apart(act, const, t_full, m)
                        nc.scalar.activation(yT[:], Y[:, par, :], ACT.Identity,
                                             bias=B2[:, bass.ds(e, 1)]).then_inc(y_done, 1)

                act.wait_ge(b_loaded, 32)
                walk(act, do)

            @block.tensor
            def _(pe):
                class do:
                    finish_at = 2
                    @staticmethod
                    def next_weights(e, ep):
                        pe.wait_ge(w_split, 4 * (e + 1))

                    @staticmethod
                    def up(n, slot, c, blk, e, ep):
                        need(pe, g_done, n - 2)
                        for half in range(2):
                            w = [W[:, ep, half * H + c * P:half * H + (c + 1) * P] for W in W1]
                            last = passes(nc, U[:, slot, half, :], w, [x[:, bass.ds(blk * BT, BT)] for x in XT])
                        last.then_inc(u_full, 1)

                    gate = staticmethod(nothing)

                    @staticmethod
                    def down(n, q, c, m, par, e, ep):
                        pe.wait_ge(l_done, n + 1)
                        if c == 0:
                            need(pe, x_done, GB * (m - 1))
                        passes(nc, Y[:, par, :], [W[:, ep, c * P:(c + 1) * P] for W in W2],
                               [g[:, q, :] for g in GP], start=c == 0, stop=c == NC - 1).then_inc(d_done, 1)

                    @staticmethod
                    def finish(m, par, blk, e):
                        pe.wait_ge(y_done, m + 1)
                        for j in range(GB):
                            last = pe.transpose(Y[:, par, j * P:(j + 1) * P], yT[:, j * P:(j + 1) * P],
                                                const.ident[:])
                        last.then_inc(t_full, 1)

                walk(pe, do)


def build(nc, a, out):
    with ExitStack() as ctx:
        X = ctx.enter_context(nc.sbuf_tensor("X", [P, NB, P], F32))
        MV = ctx.enter_context(nc.sbuf_tensor("MV", [P, NB, 2], F32))
        const = Constants(nc, ctx, a["identity"])
        for layer in range(2):
            w = f"L{layer}_xattn_"
            attention(nc, const, X, MV, layer, a["x"] if layer == 0 else None, a["ctx_1024"],
                      a["mask_BxSxS2_bk1"], a[w + "Wq"], a[w + "Wk"], a[w + "Wv"], a[w + "Wo"],
                      a[w + "bo"], a["signs"])
            with ExitStack() as ffn:
                XT = [ffn.enter_context(nc.sbuf_tensor(f"XT{layer}{i}", [P, NB * P], F32R)) for i in range(2)]
                LG = ffn.enter_context(nc.sbuf_tensor(f"LG{layer}", [P, NB, NE], F32))
                if layer == 0:
                    normalise_all(nc, const, X, MV, 0, XT, LG, a["L0_ffn_gate_w"], a["L0_ffn_gate_b"])
                    scale = ffn.enter_context(nc.sbuf_tensor("scale", [P, NB], F32))
                    gate_scale(nc, LG, scale, a["L0_ffn_rms_w"])
                    dense_experts(nc, const, X, XT, scale, a["L0_ffn_w1"], a["L0_ffn_b1"], a["L0_ffn_w2"],
                                  a["L0_ffn_b2"])
                else:
                    normalise_all(nc, const, X, MV, 1, XT, LG, a["L1_ffn_router_w"], a["L1_ffn_router_b"])
                    WT = ffn.enter_context(nc.sbuf_tensor("WT", [P, NB, NE], F32))
                    top2_weights(nc, LG, WT, a["rank"])
                    routed_experts(nc, const, X, XT, WT, a["L1_ffn_w1"], a["L1_ffn_b1"], a["L1_ffn_w2"],
                                   a["L1_ffn_b2"], out)


def kernel(**inputs):
    import numpy as np
    import concourse.bacc as bacc
    from concourse.bass_utils import run_bass_kernel_spmd

    def turned(a, *order):
        return np.ascontiguousarray(np.transpose(a, order))

    a = {k: np.asarray(v) for k, v in inputs.items()}
    for name in ("Wq", "Wk", "Wv", "Wo"):
        a[f"L0_xattn_{name}"] = turned(a[f"L0_xattn_{name}"], 1, 0)
    a["L0_ffn_gate_w"] = turned(a["L0_ffn_gate_w"], 1, 0)
    a["L1_ffn_router_w"] = turned(a["L1_ffn_router_w"], 1, 0)
    a["L1_ffn_w1"] = turned(a["L1_ffn_w1"], 0, 2, 1)
    a["L1_ffn_w2"] = turned(a["L1_ffn_w2"], 0, 2, 1)
    for layer in range(2):
        b1 = a[f"L{layer}_ffn_b1"]
        a[f"L{layer}_ffn_b1"] = turned(b1.reshape(-1, P), 1, 0)
        a[f"L{layer}_ffn_b2"] = turned(a[f"L{layer}_ffn_b2"], 1, 0)
    row = np.arange(P) % 32 // 8
    a["identity"] = np.eye(P, dtype=np.float32)
    a["signs"] = np.stack([row >= 2, row % 2 == 1], 1).astype(np.float32)
    a["rank"] = np.arange(NE, 0, -1, dtype=np.float32)
    a = {k: np.ascontiguousarray(v) for k, v in a.items()}

    nc = bacc.Bacc("TRN2", target_bir_lowering=False, num_devices=1)
    aps = {k: nc.dram_tensor(k, v.shape, mybir.dt.from_np(v.dtype), kind="ExternalInput").ap() for k, v in a.items()}
    out = nc.dram_tensor("out", (NB, P, P), F32, kind="ExternalOutput").ap()
    build(nc, aps, out)
    r = run_bass_kernel_spmd(nc, [a], core_ids=[0])
    return r.results[0]["out"]
```
